# Optimizing a Trainium2 kernel written in Bass

```python
import numpy as np
import jax
import jax.numpy as jnp

def _softmax(x, axis=-1):
    return jax.nn.softmax(x, axis=axis)

def _gelu(x):
    return jax.nn.gelu(x, approximate=True)

def _silu(x):
    return jax.nn.silu(x)

def _sigmoid(x):
    return jax.nn.sigmoid(x)

def _layernorm(x, axis=-1, eps=1e-05):
    m = jnp.mean(x, axis=axis, keepdims=True)
    v = jnp.var(x, axis=axis, keepdims=True)
    return (x - m) / jnp.sqrt(v + eps)

def _scatter_add(tgt, idx, src, axis=0):
    return tgt.at[idx].add(src)

def _segment_sum(src, seg, n):
    return jax.ops.segment_sum(src, seg, n)
kernel_name = 'mk_adaln_ffn_d1_seqx_r4_d19bf0'

def setup_inputs(seed: int=0):
    np.random.seed(seed)
    _w = jnp.asarray

    def _rec_inputs():
        import jax
        import jax.numpy as jnp
        _rk = jax.random.key(seed)
        x = -0.0003929 + 0.9999 * jax.random.normal(jax.random.fold_in(_rk, 1), (128, 64, 1024), jnp.float32)
        _lenS = 64 - jax.random.randint(jax.random.fold_in(_rk, 7), (128,), 0, max(1, 64 // 4) + 1, jnp.int32)
        _lenS2 = 64 - jax.random.randint(jax.random.fold_in(_rk, 8), (128,), 0, max(1, 64 // 4) + 1, jnp.int32)
        itok_B_8_3872 = jax.random.randint(jax.random.fold_in(_rk, 11), (128,), 8, 3873, jnp.int32)
        return (x, itok_B_8_3872)
    x, itok_B_8_3872 = _rec_inputs()

    def _L0_cond_setup():
        import math
        import jax, jax.numpy as jnp
        import numpy as np
        H, N, B, L = (64, 64, 16, 1024)
        DT_MIN, DT_MAX = (0.001, 0.1)

        def _get_kernel(log_dt, C, log_A_real, A_imag, length):
            Cc = C[..., 0] + 1j * C[..., 1]
            dt = jnp.exp(log_dt)
            A = -jnp.exp(log_A_real) + 1j * A_imag
            dtA = A * dt[:, None]
            P = dtA[:, :, None] * jnp.arange(length, dtype=jnp.float32)
            Cs = Cc * (jnp.exp(dtA) - 1.0) / A
            K = 2.0 * jnp.einsum('hn,hnl->hl', Cs, jnp.exp(P)).real
            return K
        key = jax.random.key(seed)
        ks = jax.random.split(key, 6)
        u = jax.random.normal(ks[0], (B, H, L), dtype=jnp.float32)
        length = jax.random.randint(ks[1], (B,), 0, L)
        log_dt = jax.random.uniform(ks[2], (H,), dtype=jnp.float32) * (math.log(DT_MAX) - math.log(DT_MIN)) + math.log(DT_MIN)
        C = jax.random.normal(ks[3], (H, N, 2), dtype=jnp.float32)
        log_A_real = jnp.log(0.5 * jnp.ones((H, N), dtype=jnp.float32))
        A_imag = math.pi * jnp.broadcast_to(jnp.arange(N, dtype=jnp.float32), (H, N))
        D = jax.random.normal(ks[4], (H,), dtype=jnp.float32)
        return {'u': u, 'length': length, 'log_dt': log_dt, 'C': C, 'log_A_real': log_A_real, 'A_imag': A_imag, 'D': D}
    _L0_cond_all = _L0_cond_setup()
    _L0_cond_in = {k: v for k, v in _L0_cond_all.items() if k in ('log_dt', 'C', 'log_A_real', 'A_imag', 'D')}
    del _L0_cond_all

    def _L0_ffn_setup():
        import jax, jax.numpy as jnp
        import numpy as np
        NUM_EXPERTS = 8
        TOP_K = 2
        RANK = 16
        LORA_ALPHA = 32
        SCALING = LORA_ALPHA / RANK
        key = jax.random.key(seed)
        ks = jax.random.split(key, 6)
        B, S, D_IN, D_OUT = (4, 512, 1024, 1024)
        x = jax.random.normal(ks[0], (B, S, D_IN), dtype=jnp.float32)
        W_base = jax.random.normal(ks[1], (D_OUT, D_IN), dtype=jnp.float32) * 0.02
        b_base = jax.random.normal(ks[2], (D_OUT,), dtype=jnp.float32) * 0.02
        W_router = jax.random.normal(ks[3], (NUM_EXPERTS, D_IN), dtype=jnp.float32) * 0.02
        A = jax.random.normal(ks[4], (NUM_EXPERTS, RANK, D_IN), dtype=jnp.float32) * 0.02
        Bm = jax.random.normal(ks[5], (D_OUT, RANK), dtype=jnp.float32) * 0.02
        Bm = jnp.broadcast_to(Bm, (NUM_EXPERTS, D_OUT, RANK)) * jnp.arange(1, NUM_EXPERTS + 1, dtype=jnp.float32)[:, None, None] * 0.2
        return {'x': x, 'W_base': W_base, 'b_base': b_base, 'W_router': W_router, 'A': A, 'B': Bm}
    _L0_ffn_all = _L0_ffn_setup()
    _L0_ffn_in = {k: v for k, v in _L0_ffn_all.items() if k in ('W_base', 'b_base', 'W_router', 'A', 'B')}
    del _L0_ffn_all
    return {'x': x, 'itok_B_8_3872': itok_B_8_3872, 'L0_cond_log_dt': _L0_cond_in['log_dt'], 'L0_cond_C': _L0_cond_in['C'], 'L0_cond_log_A_real': _L0_cond_in['log_A_real'], 'L0_cond_A_imag': _L0_cond_in['A_imag'], 'L0_cond_D': _L0_cond_in['D'], 'L0_ffn_W_base': _L0_ffn_in['W_base'], 'L0_ffn_b_base': _L0_ffn_in['b_base'], 'L0_ffn_W_router': _L0_ffn_in['W_router'], 'L0_ffn_A': _L0_ffn_in['A'], 'L0_ffn_B': _L0_ffn_in['B']}

def reference(x, itok_B_8_3872, L0_cond_log_dt, L0_cond_C, L0_cond_log_A_real, L0_cond_A_imag, L0_cond_D, L0_ffn_W_base, L0_ffn_b_base, L0_ffn_W_router, L0_ffn_A, L0_ffn_B):
    import jax
    import jax.numpy as jnp

    def _L0_cond_ref(u, length, log_dt, C, log_A_real, A_imag, D):
        import math
        import jax, jax.numpy as jnp
        import numpy as np
        H, N, B, L = (64, 64, 16, 1024)
        DT_MIN, DT_MAX = (0.001, 0.1)

        def _get_kernel(log_dt, C, log_A_real, A_imag, length):
            Cc = C[..., 0] + 1j * C[..., 1]
            dt = jnp.exp(log_dt)
            A = -jnp.exp(log_A_real) + 1j * A_imag
            dtA = A * dt[:, None]
            P = dtA[:, :, None] * jnp.arange(length, dtype=jnp.float32)
            Cs = Cc * (jnp.exp(dtA) - 1.0) / A
            K = 2.0 * jnp.einsum('hn,hnl->hl', Cs, jnp.exp(P)).real
            return K
        Bq, Hq, Lq = u.shape
        mask = (jnp.arange(Lq) < length[:, None]).astype(u.dtype)
        u_m = u * mask[:, None, :]
        kernel = _get_kernel(log_dt, C, log_A_real, A_imag, Lq)
        n = 2 * Lq
        k_f = jnp.fft.rfft(kernel, n=n)
        u_f = jnp.fft.rfft(u_m, n=n)
        y = jnp.fft.irfft(u_f * k_f, n=n)[..., :Lq]
        y = y + u_m * D[:, None]
        return y * mask[:, None, :]

    def _L0_ffn_ref(x, W_base, b_base, W_router, A, B):
        import jax, jax.numpy as jnp
        import numpy as np
        NUM_EXPERTS = 8
        TOP_K = 2
        RANK = 16
        LORA_ALPHA = 32
        SCALING = LORA_ALPHA / RANK
        bs, seq, d_in = x.shape
        T = bs * seq
        xf = x.reshape(T, d_in)
        base = xf @ W_base.T + b_base
        logits = xf @ W_router.T
        rw, sel = jax.lax.top_k(logits, TOP_K)
        rw = jax.nn.softmax(rw, axis=-1)
        onehot = jax.nn.one_hot(sel, NUM_EXPERTS, dtype=rw.dtype)
        w = jnp.einsum('tk,tke->te', rw, onehot)
        h = jnp.einsum('td,erd->ter', xf, A)
        lora = jnp.einsum('ter,te,eor->to', h, w, B) * SCALING
        return (base + lora).reshape(bs, seq, -1)
    x = x + _L0_ffn_ref(_L0_cond_ref(x, itok_B_8_3872, L0_cond_log_dt, L0_cond_C, L0_cond_log_A_real, L0_cond_A_imag, L0_cond_D), L0_ffn_W_base, L0_ffn_b_base, L0_ffn_W_router, L0_ffn_A, L0_ffn_B)
    return x

_drawn_inputs = setup_inputs


def setup_inputs(seed=0):
    import zlib

    import numpy as np

    out = dict(_drawn_inputs(seed))
    spreads = {'L0_cond_log_A_real': (-0.6931471824645996, 0.2)}
    factors = {'L0_ffn_b_base': 4.058}
    for name, (base, spread) in spreads.items():
        noise = np.random.default_rng([zlib.crc32(name.encode()), seed]).standard_normal(out[name].shape)
        drawn = base * np.exp(spread * noise) if base else spread * noise
        out[name] = jnp.asarray(drawn.astype(out[name].dtype))
    for name, factor in factors.items():
        out[name] = (out[name] * factor).astype(out[name].dtype)
    return out
```

```python
from contextlib import ExitStack
import math

import numpy as np
import concourse.bass as bass
from concourse import mybir

F32 = mybir.dt.float32
F32R = mybir.dt.float32r
I32 = mybir.dt.int32
AX_X = mybir.AxisListType.X
ALU = mybir.AluOpType
ACT = mybir.ActivationFunctionType

P = 128
BANK = 512
MAGIC = 1.5 * 2.0 ** 23
LOG2E = 1.0 / math.log(2.0)
LN2_HI = 0.693359375
LN2_LO = math.log(2.0) - LN2_HI
TWO_PI_1 = 6.28125
TWO_PI_2 = math.floor((2 * math.pi - TWO_PI_1) * 2.0 ** 20) / 2.0 ** 20
TWO_PI_3 = 2 * math.pi - TWO_PI_1 - TWO_PI_2
PI_BELOW = 3.1415925


def s4d_lora_ffn(nc, x, lengths, log_dt, C, log_A_real, A_imag, D, W_base, b_base, W_router, A_lora, B_lora, out):
    B, H, L = x.shape
    N = A_imag.shape[1]
    E, R, _ = A_lora.shape
    O = W_base.shape[0]
    ER = E * R
    NC = L // P
    HALF = NC // 2
    HC = HALF * P
    assert B == P and ER == P and 2 * N == P and HC == BANK and O == L and H % 4 == 0
    SCALING = 32.0 / R
    COLS = O + ER + E
    SEG = [0, 388, 776, COLS]
    LSEG = [0, 388, 776, O]
    A0, R0 = O - SEG[2], O + ER - SEG[2]
    PW = 32
    NA = L // PW
    HP = H // 2
    Q4 = P // NA
    H8 = HP // Q4
    PAD = P
    ROW = PAD + L
    XS = 4
    TS = 2
    UNROLL = 4
    ROUTE_STEPS = 10

    k_dram = nc.dram_tensor("k_split_dram", [H, 2, ROW], F32, kind="Internal")

    with ExitStack() as ctx:
        def sb(name, shape, dt):
            return ctx.enter_context(nc.sbuf_tensor(name, shape, dt))

        def sem(name):
            return ctx.enter_context(nc.semaphore(name))

        w_hi = sb("w_hi", [P, NC, COLS], F32R)
        w_lo = sb("w_lo", [P, NC, COLS], F32R)
        b2_hi = sb("b2_hi", [P, O], F32R)
        b2_lo = sb("b2_lo", [P, O], F32R)
        bias_rows = sb("bias_rows", [P, O], F32)
        mask_rows = sb("mask_rows", [P, L], F32)
        mask_cols = sb("mask_cols", [P, NC, P], F32)
        ident = sb("ident", [P, P], F32)
        lower = sb("lower", [P, E, E], F32)
        rank_limit = sb("rank_limit", [P, E], F32)
        half_pi = sb("half_pi", [P, 1], F32)
        x_slot = sb("x_slot", [P, XS, L], F32)
        xm = sb("xm", [P, L], F32)
        u_hi = sb("u_hi", [P, NC, P], F32R)
        u_lo = sb("u_lo", [P, NC, P], F32R)
        ym = sb("ym", [P, NC, P], F32)
        y_hi = sb("y_hi", [P, NC, P], F32R)
        y_lo = sb("y_lo", [P, NC, P], F32R)
        toep = sb("toep", [P, TS, 2, L], F32R)
        logit = sb("logit", [P, E], F32)
        top = sb("top", [P, 1], F32)
        below = sb("below", [P, E], F32)
        weight = sb("weight", [P, E], F32)
        before = sb("before", [P, E, E], F32)
        balance = sb("balance", [P, E, E], F32)
        rank = sb("rank", [P, E], F32)
        gate = sb("gate", [P, E], F32)
        total = sb("total", [P, 1], F32)
        hw = sb("hw", [P, E, R], F32)
        hwt_hi = sb("hwt_hi", [P, P], F32R)
        hwt_lo = sb("hwt_lo", [P, P], F32R)
        w_stage = sb("w_stage", [P, 2, L], F32)
        theta = sb("theta", [P, HP, 2 * PW], F32)
        turns = sb("turns", [P, HP, 2 * PW], F32)
        magn = sb("magn", [P, HP, 2 * PW], F32)
        tab_re = sb("tab_re", [P, HP, 2 * PW], F32)
        tab_im = sb("tab_im", [P, HP, 2 * PW], F32)
        pos = sb("pos", [P, 2, PW], F32)
        coef = sb("coef", [P, 4, HP], F32)
        nat4 = sb("nat4", [N, 4, 2, N], F32)
        lin = sb("lin", [H, N + 1], F32)
        aim = sb("aim", [H, N], F32)
        cc = sb("cc", [H, N, 2], F32)
        small = [sb(f"small{i}", [H, N + 1], F32) for i in range(10)]
        ki = sb("ki", [H, N + 1], I32)
        len_col = sb("len_col", [P, 1], I32)
        len_colf = sb("len_colf", [P, 1], F32)
        len_row = sb("len_row", [P, P], I32)
        len_rowf = sb("len_rowf", [P, P], F32)
        chunk_pos = sb("chunk_pos", [P, NC], F32)
        d_tile = sb("d_tile", [P, H], F32)
        xm_reversed = bass.AP(xm, P - 1, [[L, P], [P, NC], [-1, P]])
        kf = ym[:, 0:HALF, :].rearrange("p c n -> p (c n)").rearrange("p (a h n) -> p a h n", a=2, h=H8)
        zeros = y_hi[0:H, 0:2, :]
        k_split = y_lo[:].rearrange("p c n -> p (c n)").rearrange("p (s a h n) -> p s a h n", s=2, a=2, h=H8)

        ps_base = [ctx.enter_context(nc.psum_tensor(f"ps_base{s}", [P, BANK], F32)) for s in range(3)]
        ps_y = [ctx.enter_context(nc.psum_tensor(f"ps_y{s}", [P, BANK], F32)) for s in range(2)]
        ps_u = [ctx.enter_context(nc.psum_tensor(f"ps_u{s}", [P, BANK], F32)) for s in range(2)]
        ps_h = ctx.enter_context(nc.psum_tensor("ps_h", [P, BANK], F32))

        params_in = sem("params_in")
        lens_in = sem("lens_in")
        bias_in = sem("bias_in")
        d_in = sem("d_in")
        stage_in = [sem(f"stage_in{i}") for i in range(4)]
        router_in = sem("router_in")
        const_ready = sem("const_ready")
        zeros_ready = sem("zeros_ready")
        lens_float = sem("lens_float")
        masks_ready = sem("masks_ready")
        pool_chain = sem("pool_chain")
        dve_chain = sem("dve_chain")
        half_angle = sem("half_angle")
        half_sin = sem("half_sin")
        nat_ready = sem("nat_ready")
        nat_turned = sem("nat_turned")
        coef_ready = sem("coef_ready")
        decay_arg = sem("decay_arg")
        decay_ready = sem("decay_ready")
        angle_ready = sem("angle_ready")
        sincos_ready = sem("sincos_ready")
        tables_ready = sem("tables_ready")
        k_done = sem("k_done")
        k_ready = sem("k_ready")
        k_stored = sem("k_stored")
        wt_turned = sem("wt_turned")
        wt_hi_ready = sem("wt_hi_ready")
        wt_lo_ready = sem("wt_lo_ready")
        x_loaded = [sem(f"x_loaded{i}") for i in range(XS)]
        toep_loaded = [sem(f"toep_loaded{i}") for i in range(TS)]
        stored = [sem(f"stored{i}") for i in range(XS)]
        x_masked = sem("x_masked")
        x_biased = sem("x_biased")
        u_turned = sem("u_turned")
        u_hi_ready = sem("u_hi_ready")
        u_lo_ready = sem("u_lo_ready")
        conv_done = sem("conv_done")
        y_masked = sem("y_masked")
        y_hi_ready = sem("y_hi_ready")
        y_lo_ready = sem("y_lo_ready")
        base_done = sem("base_done")
        route_chain = sem("route_chain")
        below_ready = sem("below_ready")
        weight_ready = sem("weight_ready")
        hw_ready = sem("hw_ready")
        hw_turned = sem("hw_turned")
        hwt_hi_ready = sem("hwt_hi_ready")
        hwt_lo_ready = sem("hwt_lo_ready")
        lora_done = sem("lora_done")
        out_ready = [sem(f"out_ready{s}") for s in range(3)]

        NB = O // P
        stage = [w_stage[:, 0, :], w_stage[:, 1, :], x_slot[:, 2, :], x_slot[:, 3, :]]
        router_stage = xm[0:E, :]
        blocks = [(W_base[P * i:P * (i + 1), :], P * i) for i in range(NB)]
        blocks.append((A_lora.rearrange("e r d -> (e r) d"), O))
        units = [(stage[i % 4], col, c0, P) for i, (_, col) in enumerate(blocks) for c0 in (0, HALF)]
        B_UNIT = len(units)
        NUNITS = B_UNIT + 3
        b_slot = len(blocks) % 4
        unit_bank = [ps_y[0], ps_y[1], ps_u[0], ps_u[1]]
        EARLY = 4

        def weight_unit(eng, u):
            if u >= 4:
                eng.wait_ge(wt_hi_ready, u - 3)
                eng.wait_ge(wt_lo_ready, u - 3)
            bank = unit_bank[u % 4]
            if u < B_UNIT:
                src, _, c0, _ = units[u]
                blk = u // 2
                eng.wait_ge(stage_in[blk % 4], 16 * (blk // 4 + 1))
                for k in range(HALF):
                    mm = eng.transpose(bank[:, k * P:(k + 1) * P], src[:, (c0 + k) * P:(c0 + k + 1) * P], ident[:])
            elif u < B_UNIT + 2:
                half = u - B_UNIT
                eng.wait_ge(stage_in[b_slot], 16 * (len(blocks) // 4) + 16 * E)
                for k in range(HALF):
                    c = half * HALF + k
                    mm = eng.transpose(bank[:, k * P:(k + 1) * P], stage[b_slot][:, c * P:(c + 1) * P], ident[:])
            else:
                eng.wait_ge(router_in, 16)
                for c in range(NC):
                    mm = eng.transpose(bank[:, c * E:(c + 1) * E], router_stage[:, c * P:(c + 1) * P],
                                       ident[0:E, 0:E])
            mm.then_inc(wt_turned, 1)

        def unit_views(u):
            bank = unit_bank[u % 4]
            if u < B_UNIT:
                _, col, c0, n = units[u]
                src = bank[:].rearrange("p (c n) -> p c n", c=HALF)
                return src, w_hi[:, c0:c0 + HALF, col:col + n], w_lo[:, c0:c0 + HALF, col:col + n], 1.0
            if u < B_UNIT + 2:
                at = (u - B_UNIT) * HC
                return bank[:], b2_hi[:, at:at + HC], b2_lo[:, at:at + HC], SCALING
            src = bank[:, 0:NC * E].rearrange("p (c n) -> p c n", c=NC)
            return src, w_hi[:, :, O + ER:COLS], w_lo[:, :, O + ER:COLS], 1.0

        def weight_hi(eng, u):
            eng.wait_ge(wt_turned, u + 1)
            src, hi, _, factor = unit_views(u)
            eng.activation(hi, src, ACT.Copy, scale=factor).then_inc(wt_hi_ready, 1)

        def weight_lo(eng, u):
            eng.wait_ge(wt_hi_ready, u + 1)
            src, hi, lo, factor = unit_views(u)
            eng.scalar_tensor_tensor(out=lo, in0=src, scalar=factor, in1=hi.bitcast(F32),
                                     op0=ALU.mult, op1=ALU.subtract).then_inc(wt_lo_ready, 1)

        def toeplitz_source(h):
            return bass.AP(k_dram, h * (2 * ROW) + PAD - (P - 1), [[1, P], [ROW, 2], [1, L]])

        block = ctx.enter_context(nc.Block())

        @block.sync
        def _(sp):
            sp.dma_start(lin[:, 0:N], log_A_real).then_inc(params_in, 16)
            sp.dma_start(lin[:, N:N + 1], log_dt.rearrange("(h o) -> h o", o=1)).then_inc(params_in, 16)
            sp.dma_start(aim[:], A_imag).then_inc(params_in, 16)
            sp.dma_start(cc[:], C).then_inc(params_in, 16)
            sp.dma_start(len_col[:], lengths.rearrange("(b o) -> b o", o=1)).then_inc(lens_in, 16)
            sp.dma_start(len_row[:], bass.AP(lengths.tensor, 0, [[0, P], [1, B]])).then_inc(lens_in, 16)
            for i in range(2):
                sp.dma_start(stage[i], blocks[i][0]).then_inc(stage_in[i], 16)
            for h in range(2):
                sp.dma_start(x_slot[:, h, :], x[:, h, :]).then_inc(x_loaded[h], 16)
            for i in range(2, 4):
                sp.dma_start(stage[i], blocks[i][0]).then_inc(stage_in[i], 16)
            sp.dma_start(router_stage, W_router).then_inc(router_in, 16)
            sp.dma_start(bias_rows[:], bass.AP(b_base.tensor, 0, [[0, P], [1, O]])).then_inc(bias_in, 16)
            for q in range(Q4):
                sp.dma_start(d_tile[NA * q:NA * q + 1, :], D.rearrange("(o h) -> o h", o=1)).then_inc(d_in, 16)
            sp.wait_ge(zeros_ready, 1)
            sp.dma_start(bass.AP(k_dram, 0, [[2 * ROW, H], [ROW, 2], [1, PAD]]), zeros.bitcast(F32)).then_inc(k_stored, 16)
            for i in range(4, 4 + EARLY // 2):
                sp.wait_ge(wt_turned, 2 * (i - 4) + 2)
                sp.dma_start(stage[i % 4], blocks[i][0]).then_inc(stage_in[i % 4], 16)
            sp.wait_ge(k_ready, 2)
            for q in range(Q4):
                for part in range(2):
                    for par in range(2):
                        dst = bass.AP(k_dram, (2 * q + par) * 2 * ROW + part * ROW + PAD,
                                      [[PW, NA], [2 * Q4 * 2 * ROW, H8], [1, PW]])
                        sp.dma_start(dst, k_split[NA * q:NA * (q + 1), part, par, :, :].bitcast(F32)).then_inc(k_stored, 16)
            sp.wait_ge(k_stored, 16 * (4 * Q4 + 1))
            for h in range(TS):
                sp.dma_start(toep[:, h, :, :].bitcast(F32), toeplitz_source(h)).then_inc(toep_loaded[h], 16)
            for i in range(4 + EARLY // 2, len(blocks)):
                sp.wait_ge(wt_turned, 2 * (i - 4) + 2)
                sp.dma_start(stage[i % 4], blocks[i][0]).then_inc(stage_in[i % 4], 16)
            i = len(blocks)
            sp.wait_ge(wt_turned, 2 * (i - 4) + 2)
            for e in range(E):
                dst = stage[b_slot].rearrange("p (c e r) -> p c e r", c=NB, e=E)[:, :, e, :]
                sp.dma_start(dst, B_lora[e].rearrange("(c p) r -> p c r", p=P)).then_inc(stage_in[b_slot], 16)
            sp.wait_ge(wt_turned, B_UNIT + 2)
            for h in range(2, XS):
                sp.dma_start(x_slot[:, h, :], x[:, h, :]).then_inc(x_loaded[h], 16)

            with sp.Fori(0, H // UNROLL - 1) as t:
                for j in range(UNROLL):
                    i = UNROLL * t + j
                    sp.wait_ge(conv_done, 2 * i + 2)
                    sp.dma_start(toep[:, j % TS, :, :].bitcast(F32), toeplitz_source(i + TS)).then_inc(toep_loaded[j % TS], 16)
                    for s in range(3):
                        sp.wait_ge(out_ready[s], i + 1)
                    sp.dma_start(out[:, i, :], x_slot[:, j, :]).then_inc(stored[j], 16)
                    sp.wait_ge(stored[j], 16 * t + 16)
                    sp.dma_start(x_slot[:, j, :], x[:, i + XS, :]).then_inc(x_loaded[j], 16)
            for j in range(UNROLL):
                i = H - UNROLL + j
                if i + TS < H:
                    sp.wait_ge(conv_done, 2 * i + 2)
                    sp.dma_start(toep[:, j % TS, :, :].bitcast(F32), toeplitz_source(i + TS)).then_inc(toep_loaded[j % TS], 16)
                for s in range(3):
                    sp.wait_ge(out_ready[s], i + 1)
                sp.dma_start(out[:, i, :], x_slot[:, j, :]).then_inc(stored[j], 16)
            for j in range(XS):
                sp.wait_ge(stored[j], 16 * (H // XS))

        @block.gpsimd
        def _(pool):
            count = [0]

            def link(ins):
                count[0] += 1
                ins.then_inc(pool_chain, 1)
                pool.wait_ge(pool_chain, count[0])

            pool.memset(zeros.bitcast(F32), 0.0).then_inc(zeros_ready, 1)
            link(pool.memset(ident[:], 0.0))
            pool.affine_select(out=ident[:], in_=ident[:], compare_op=ALU.not_equal, fill=1.0, base=0,
                               pattern=[[-1, P]], channel_multiplier=1).then_inc(const_ready, 1)
            pool.memset(half_pi[:], math.pi / 2).then_inc(const_ready, 1)
            pool.iota(pos[:, 0, :], [[1, PW]], base=0, channel_multiplier=0,
                      allow_small_or_imprecise_dtypes=True).then_inc(const_ready, 1)
            pool.iota(pos[:, 1, :], [[PW, NA]], base=0, channel_multiplier=0,
                      allow_small_or_imprecise_dtypes=True).then_inc(const_ready, 1)
            pool.iota(chunk_pos[:], [[P, NC]], base=0, channel_multiplier=1,
                      allow_small_or_imprecise_dtypes=True).then_inc(const_ready, 1)
            pool.iota(rank_limit[:], [[1, E]], base=3 - E, channel_multiplier=0,
                      allow_small_or_imprecise_dtypes=True).then_inc(const_ready, 1)
            link(pool.memset(lower[:], 1.0))
            pool.affine_select(out=lower[:], in_=lower[:], compare_op=ALU.is_gt, fill=0.0, base=0,
                               pattern=[[1, E], [-1, E]], channel_multiplier=0).then_inc(const_ready, 1)
            link(pool.iota(mask_rows[:], [[1, L]], base=0, channel_multiplier=0,
                           allow_small_or_imprecise_dtypes=True))
            pool.wait_ge(lens_float, 2)
            link(pool.tensor_scalar(mask_rows[:], mask_rows[:], len_colf[:, 0:1], None, ALU.is_lt))
            for c in range(NC):
                ins = pool.tensor_scalar(mask_cols[:, c, :], len_rowf[:], chunk_pos[:, c:c + 1], None, ALU.is_gt)
                ins.then_inc(masks_ready, 1)
            pool.wait_ge(coef_ready, 2)
            pool.tensor_tensor(
                magn[:],
                coef[:, 0, :].unsqueeze(2).broadcast_to([P, HP, 2 * PW]),
                pos[:].rearrange("p k n -> p (k n)").unsqueeze(1).broadcast_to([P, HP, 2 * PW]),
                ALU.mult).then_inc(decay_arg, 1)

            def mask_x(i, j, loads):
                pool.wait_ge(x_loaded[j], loads)
                pool.tensor_tensor(xm_reversed, x_slot[:, j, :].rearrange("p (c n) -> p c n", c=NC),
                                   mask_rows[:].rearrange("p (c n) -> p c n", c=NC),
                                   ALU.mult).then_inc(x_masked, 1)
                pool.wait_ge(x_masked, i + 1)
                pool.tensor_tensor(x_slot[:, j, :], x_slot[:, j, :], bias_rows[:], ALU.add).then_inc(x_biased, 1)

            pool.wait_ge(wt_turned, NUNITS)
            pool.wait_ge(bias_in, 16)
            mask_x(0, 0, 16)
            for h in (1, 2):
                pool.wait_ge(u_turned, 2 * h)
                mask_x(h, h, 16)
            with pool.Fori(0, H // UNROLL - 1) as t:
                for j in range(UNROLL):
                    i = UNROLL * t + j
                    k = (j + 3) % XS
                    pool.wait_ge(u_turned, 2 * i + 6)
                    mask_x(i + 3, k, 16 * t + 16 + 16 * ((j + 3) // XS))
            i = H - UNROLL
            pool.wait_ge(u_turned, 2 * i + 6)
            mask_x(i + 3, (i + 3) % XS, 16 * (H // XS))

        @block.scalar
        def _(act):
            for u in range(EARLY):
                weight_hi(act, u)
            act.wait_ge(const_ready, 2)
            act.wait_ge(half_angle, 1)
            act.activation(small[4][:, 0:N], small[2][:, 0:N], ACT.Sin, scale=0.5).then_inc(half_sin, 1)
            act.activation(small[5][:, 0:N], small[3][:, 0:N], ACT.Sin, scale=-0.5,
                           bias=half_pi[0:H, :]).then_inc(half_sin, 1)
            act.wait_ge(decay_arg, 1)
            act.activation(magn[:], magn[:], ACT.Exp).then_inc(decay_ready, 1)
            act.wait_ge(angle_ready, 1)
            act.activation(tab_im[:], theta[:], ACT.Sin).then_inc(sincos_ready, 1)
            act.wait_ge(angle_ready, 2)
            act.activation(tab_re[:], turns[:], ACT.Sin, scale=-1.0, bias=half_pi[:]).then_inc(sincos_ready, 1)
            for u in range(EARLY, NUNITS):
                weight_hi(act, u)

            def split_u(i):
                for half in range(2):
                    act.wait_ge(u_turned, 2 * i + half + 1)
                    c = slice(half * HALF, (half + 1) * HALF)
                    act.activation(u_hi[:, c, :], ps_u[half][:].rearrange("p (c n) -> p c n", c=HALF),
                                   ACT.Copy).then_inc(u_hi_ready, 1)

            def split_y(i, half):
                act.wait_ge(y_masked, 2 * i + half + 1)
                c = slice(half * HALF, (half + 1) * HALF)
                act.activation(y_hi[:, c, :], ym[:, c, :], ACT.Copy).then_inc(y_hi_ready, 1)

            def weights(i):
                act.wait_ge(below_ready, i + 1)
                act.activation(weight[:], below[:], ACT.Exp).then_inc(weight_ready, 1)

            def split_hw(i):
                act.wait_ge(hw_turned, i + 1)
                act.activation(hwt_hi[:], ps_h[:, 0:P], ACT.Copy).then_inc(hwt_hi_ready, 1)

            split_u(0)
            split_y(0, 0)
            split_y(0, 1)
            split_u(1)

            def head(i, ahead1=True, ahead2=True):
                weights(i)
                if ahead1:
                    split_y(i + 1, 0)
                split_hw(i)
                if ahead1:
                    split_y(i + 1, 1)
                if ahead2:
                    act.wait_ge(conv_done, 2 * i + 4)
                    split_u(i + 2)

            with act.Fori(0, H // UNROLL - 1) as t:
                for j in range(UNROLL):
                    head(UNROLL * t + j)
            for i in range(H - UNROLL, H):
                head(i, i + 1 < H, i + 2 < H)

        @block.vector
        def _(dve):
            count = [0]

            def link(ins):
                count[0] += 1
                ins.then_inc(dve_chain, 1)
                dve.wait_ge(dve_chain, count[0])

            def ts(o, i, s1, s2, op0, op1):
                link(dve.tensor_scalar(o, i, s1, s2, op0, op1))

            def tt(o, a, b, op):
                link(dve.tensor_tensor(o, a, b, op))

            def stt(o, a, s, b, op0, op1):
                link(dve.scalar_tensor_tensor(out=o, in0=a, scalar=s, in1=b, op0=op0, op1=op1))

            def exponential(v, n, e_out, em1_out, k, r, p):
                ts(r, v, -87.0, 88.0, ALU.max, ALU.min)
                ts(k, r, LOG2E, MAGIC, ALU.mult, ALU.add)
                ts(k, k, -MAGIC, None, ALU.add, ALU.bypass)
                stt(r, k, -LN2_HI, r, ALU.mult, ALU.add)
                stt(r, k, -LN2_LO, r, ALU.mult, ALU.add)
                ts(p, r, 1.0 / 5040, None, ALU.mult, ALU.bypass)
                for f in (720, 120, 24, 6, 2, 1):
                    stt(p, p, 1.0 / f, r, ALU.add, ALU.mult)
                ts(ki[:, 0:n], k, 127.0, 2.0 ** 23, ALU.add, ALU.mult)
                pow2 = ki[:, 0:n].bitcast(F32)
                tt(p, p, pow2, ALU.mult)
                if e_out is not None:
                    tt(e_out, p, pow2, ALU.add)
                if em1_out is not None:
                    stt(em1_out, pow2, -1.0, p, ALU.add, ALU.add)

            def reduce_angle(r, q):
                ts(q, r, 1 / (2 * math.pi), MAGIC, ALU.mult, ALU.add)
                ts(q, q, -MAGIC, None, ALU.add, ALU.bypass)
                for part in (TWO_PI_1, TWO_PI_2, TWO_PI_3):
                    stt(r, q, -part, r, ALU.mult, ALU.add)

            dve.wait_ge(lens_in, 32)
            dve.tensor_copy(len_colf[:], len_col[:]).then_inc(lens_float, 1)
            dve.tensor_copy(len_rowf[:], len_row[:]).then_inc(lens_float, 1)
            dve.wait_ge(params_in, 64)
            s = [v[:, 0:N] for v in small]
            ex = small[6]
            exponential(lin[:], N + 1, ex[:], None, small[0][:], small[1][:], small[7][:])
            mag, dt = ex[:, 0:N], ex[:, N:N + 1]
            a_nat, w_nat = nat4[:, 0, 0, :], nat4[:, 1, 0, :]
            ts(a_nat, mag, dt, -1.0, ALU.mult, ALU.mult)
            ts(w_nat, aim[:], dt, None, ALU.mult, ALU.bypass)
            ts(s[2], w_nat, 1.0, None, ALU.mult, ALU.bypass)
            reduce_angle(s[2], s[3])
            ts(s[2], s[2], -PI_BELOW, PI_BELOW, ALU.max, ALU.min)
            dve.scalar_tensor_tensor(out=s[3], in0=s[2], scalar=-1.0, in1=s[2], op0=ALU.mult, op1=ALU.max).then_inc(half_angle, 1)
            exponential(a_nat, N, None, s[8], s[0], s[1], s[7])
            dve.wait_ge(half_sin, 2)
            sn, cs, em1 = s[4], s[5], s[8]
            tt(s[0], sn, sn, ALU.mult)
            ts(s[0], s[0], -2.0, None, ALU.mult, ALU.bypass)
            stt(s[1], s[0], 1.0, em1, ALU.add, ALU.mult)
            tt(s[1], s[1], s[0], ALU.add)
            tt(s[2], sn, cs, ALU.mult)
            stt(s[2], em1, 1.0, s[2], ALU.add, ALU.mult)
            ts(s[2], s[2], 2.0, None, ALU.mult, ALU.bypass)
            c_re, c_im = cc[:, :, 0], cc[:, :, 1]
            tt(s[3], c_re, s[1], ALU.mult)
            tt(s[4], c_im, s[2], ALU.mult)
            tt(s[3], s[3], s[4], ALU.subtract)
            tt(s[4], c_re, s[2], ALU.mult)
            tt(s[5], c_im, s[1], ALU.mult)
            tt(s[4], s[4], s[5], ALU.add)
            tt(s[0], mag, mag, ALU.mult)
            tt(s[1], aim[:], aim[:], ALU.mult)
            tt(s[0], s[0], s[1], ALU.add)
            link(dve.reciprocal(s[0], s[0]))
            tt(s[1], s[4], aim[:], ALU.mult)
            tt(s[2], s[3], mag, ALU.mult)
            tt(s[1], s[1], s[2], ALU.subtract)
            tt(s[2], s[3], aim[:], ALU.mult)
            tt(s[5], s[4], mag, ALU.mult)
            stt(s[2], s[2], -1.0, s[5], ALU.mult, ALU.subtract)
            stt(nat4[:, 2, 0, :], s[1], 2.0, s[0], ALU.mult, ALU.mult)
            stt(nat4[:, 3, 0, :], s[2], 2.0, s[0], ALU.mult, ALU.mult)
            dve.tensor_copy(nat4[:, :, 1, :], nat4[:, :, 0, :]).then_inc(nat_ready, 1)
            dve.wait_ge(nat_turned, 1)
            turned = ps_h[:, 0:4 * H].rearrange("p (k h two) -> p k h two", k=4, two=2)
            dve.tensor_copy(coef[0:N, :, :], turned[0:N, :, :, 0]).then_inc(coef_ready, 1)
            dve.tensor_copy(coef[N:P, :, :], turned[N:P, :, :, 1]).then_inc(coef_ready, 1)
            dve.wait_ge(coef_ready, 2)
            dve.wait_ge(const_ready, 7)
            tt(theta[:], coef[:, 1, :].unsqueeze(2).broadcast_to([P, HP, 2 * PW]),
               pos[:].rearrange("p k n -> p (k n)").unsqueeze(1).broadcast_to([P, HP, 2 * PW]), ALU.mult)
            reduce_angle(theta[:], turns[:])
            link(dve.tensor_scalar(theta[:], theta[:], -PI_BELOW, PI_BELOW, ALU.max, ALU.min))
            dve.scalar_tensor_tensor(out=turns[:], in0=theta[:], scalar=-1.0, in1=theta[:], op0=ALU.mult,
                                     op1=ALU.max).then_inc(angle_ready, 2)
            dve.wait_ge(decay_ready, 1)
            dve.wait_ge(sincos_ready, 1)
            tt(tab_im[:], tab_im[:], magn[:], ALU.mult)
            dve.wait_ge(sincos_ready, 2)
            tt(tab_re[:], tab_re[:], magn[:], ALU.mult)
            e_re, e_im = tab_re[:, :, PW:2 * PW], tab_im[:, :, PW:2 * PW]
            x_re, x_im, tmp = theta[:, :, 0:PW], theta[:, :, PW:2 * PW], turns[:, :, 0:PW]
            k_re = coef[:, 2, :].unsqueeze(2).broadcast_to([P, HP, PW])
            k_im = coef[:, 3, :].unsqueeze(2).broadcast_to([P, HP, PW])
            tt(x_re, e_re, k_re, ALU.mult)
            tt(tmp, e_im, k_im, ALU.mult)
            tt(x_re, x_re, tmp, ALU.subtract)
            tt(x_im, e_im, k_re, ALU.mult)
            tt(tmp, e_re, k_im, ALU.mult)
            dve.scalar_tensor_tensor(out=x_im, in0=x_im, scalar=-1.0, in1=tmp, op0=ALU.mult,
                                     op1=ALU.subtract).then_inc(tables_ready, 1)
            dve.wait_ge(k_done, 1)
            for par in range(2):
                link(dve.tensor_copy(kf[:, par, :, :],
                                     ps_base[par][:, 0:H8 * PW].rearrange("p (h n) -> p h n", h=H8)))
            dve.wait_ge(d_in, 16 * Q4)
            d_view = d_tile[:].rearrange("p (g q a) -> p q a g", q=Q4, a=2)
            for q in range(Q4):
                row = slice(NA * q, NA * q + 1)
                tt(kf[row, :, :, 0], kf[row, :, :, 0], d_view[row, q], ALU.add)
            dve.tensor_copy(k_split[:, 0], kf).then_inc(k_ready, 1)
            dve.wait_ge(k_ready, 1)
            dve.tensor_tensor(k_split[:, 1], kf, k_split[:, 0].bitcast(F32), ALU.subtract).then_inc(k_ready, 1)
            for u in range(NUNITS):
                weight_lo(dve, u)

            def split_u(i):
                for half in range(2):
                    dve.wait_ge(u_hi_ready, 2 * i + half + 1)
                    c = slice(half * HALF, (half + 1) * HALF)
                    dve.tensor_tensor(u_lo[:, c, :], ps_u[half][:].rearrange("p (c n) -> p c n", c=HALF),
                                      u_hi[:, c, :].bitcast(F32), ALU.subtract).then_inc(u_lo_ready, 1)

            def mask_y(i, half):
                dve.wait_ge(conv_done, 2 * i + half + 1)
                c = slice(half * HALF, (half + 1) * HALF)
                dve.tensor_tensor(ym[:, c, :], ps_y[half][:].rearrange("p (c n) -> p c n", c=HALF),
                                  mask_cols[:, c, :], ALU.mult).then_inc(y_masked, 1)

            def split_y(i, half):
                dve.wait_ge(y_hi_ready, 2 * i + half + 1)
                c = slice(half * HALF, (half + 1) * HALF)
                dve.tensor_tensor(y_lo[:, c, :], ym[:, c, :], y_hi[:, c, :].bitcast(F32),
                                  ALU.subtract).then_inc(y_lo_ready, 1)

            def route(i):
                done = [0]

                def then(ins):
                    done[0] += 1
                    ins.then_inc(route_chain, 1)
                    dve.wait_ge(route_chain, ROUTE_STEPS * i + done[0])

                dve.wait_ge(base_done, i + 1)
                then(dve.tensor_copy(logit[:], ps_base[2][:, R0:R0 + E]))
                then(dve.tensor_reduce(top[:], logit[:], AX_X, ALU.max))
                dve.tensor_scalar(below[:], logit[:], top[:, 0:1], None, ALU.subtract).then_inc(below_ready, 1)
                then(dve.tensor_tensor(before[:], logit[:].unsqueeze(1).broadcast_to([P, E, E]),
                                       logit[:].unsqueeze(2).broadcast_to([P, E, E]), ALU.is_ge))
                then(dve.tensor_tensor(before[:], before[:], lower[:], ALU.mult))
                then(dve.tensor_tensor(balance[:], before[:], before[:].rearrange("p e f -> p f e"), ALU.subtract))
                then(dve.tensor_reduce(rank[:], balance[:], AX_X, ALU.add))
                then(dve.tensor_tensor(gate[:], rank[:], rank_limit[:], ALU.is_lt))
                dve.wait_ge(weight_ready, i + 1)
                then(dve.tensor_tensor(gate[:], gate[:], weight[:], ALU.mult))
                then(dve.tensor_reduce(total[:], gate[:], AX_X, ALU.add))
                then(dve.reciprocal(total[:], total[:]))
                assert done[0] == ROUTE_STEPS
                dve.scalar_tensor_tensor(out=hw[:], in0=ps_base[2][:, A0:A0 + ER].rearrange("p (e r) -> p e r", e=E),
                                         scalar=total[:, 0:1], in1=gate[:].unsqueeze(2).broadcast_to([P, E, R]),
                                         op0=ALU.mult, op1=ALU.mult).then_inc(hw_ready, 1)

            def split_hw(i):
                dve.wait_ge(hwt_hi_ready, i + 1)
                dve.tensor_tensor(hwt_lo[:], ps_h[:, 0:P], hwt_hi[:].bitcast(F32),
                                  ALU.subtract).then_inc(hwt_lo_ready, 1)

            def sum_out(i, j):
                dve.wait_ge(x_biased, i + 1)
                for s_ in range(3):
                    dve.wait_ge(lora_done, 3 * i + s_ + 1)
                    a, b = LSEG[s_], LSEG[s_ + 1]
                    dve.tensor_tensor(x_slot[:, j, a:b], ps_base[s_][:, 0:b - a], x_slot[:, j, a:b],
                                      ALU.add).then_inc(out_ready[s_], 1)

            dve.wait_ge(masks_ready, NC)
            split_u(0)
            mask_y(0, 0)
            split_y(0, 0)
            mask_y(0, 1)
            split_y(0, 1)
            split_u(1)

            def head(i, j, ahead1=True, ahead2=True):
                route(i)
                if ahead1:
                    mask_y(i + 1, 0)
                    split_y(i + 1, 0)
                split_hw(i)
                if ahead1:
                    mask_y(i + 1, 1)
                sum_out(i, j)
                if ahead1:
                    split_y(i + 1, 1)
                if ahead2:
                    split_u(i + 2)

            with dve.Fori(0, H // UNROLL - 1) as t:
                for j in range(UNROLL):
                    head(UNROLL * t + j, j)
            for i in range(H - UNROLL, H):
                head(i, i % XS, i + 1 < H, i + 2 < H)

        @block.tensor
        def _(pe):
            pe.wait_ge(const_ready, 1)
            for u in range(EARLY):
                weight_unit(pe, u)
            pe.wait_ge(nat_ready, 1)
            for k in range(4):
                mm = pe.transpose(ps_h[:, k * H:(k + 1) * H], nat4[:, k, :, :].rearrange("h two n -> h (two n)"),
                                  ident[0:H, 0:H])
            mm.then_inc(nat_turned, 1)
            pe.wait_ge(tables_ready, 1)
            for par in range(2):
                rows = slice(N * par, N * (par + 1))
                for hp in range(HP):
                    q, h8 = hp % Q4, hp // Q4
                    dst = ps_base[par][NA * q:NA * (q + 1), h8 * PW:(h8 + 1) * PW]
                    pe.matmul(dst, theta[rows, hp, 0:PW], tab_re[rows, hp, 0:PW], start=True, stop=False)
                    mm = pe.matmul(dst, theta[rows, hp, PW:2 * PW], tab_im[rows, hp, 0:PW], start=False, stop=True)
            mm.then_inc(k_done, 1)
            for u in range(EARLY, NUNITS):
                weight_unit(pe, u)
            pe.wait_ge(wt_lo_ready, NUNITS)

            def turn_x(i):
                pe.wait_ge(x_masked, i + 1)
                pe.wait_ge(u_hi_ready, 2 * i)
                pe.wait_ge(u_lo_ready, 2 * i)
                for half in range(2):
                    for k in range(HALF):
                        c = half * HALF + k
                        mm = pe.transpose(ps_u[half][:, k * P:(k + 1) * P], xm[:, c * P:(c + 1) * P], ident[:])
                    mm.then_inc(u_turned, 1)

            def conv_lag(j, half, d):
                j0 = max(0, half * HALF - d)
                j1 = (half + 1) * HALF - d
                o0 = (j0 + d - half * HALF) * P
                dst = ps_y[half][:, o0:BANK]
                last_d = (half + 1) * HALF - 1
                terms = ((0, u_hi), (0, u_lo), (1, u_hi))
                for n, (part, u) in enumerate(terms):
                    mm = pe.matmul(dst, toep[:, j % TS, part, d * P:(d + 1) * P], u[:, j0:j1, :],
                                   start=(d == 0 and n == 0), stop=(d == last_d and n == 2))
                return mm

            def conv(i, j, loads, middle=None):
                pe.wait_ge(toep_loaded[j % TS], loads)
                pe.wait_ge(u_hi_ready, 2 * i + 2)
                pe.wait_ge(u_lo_ready, 2 * i + 2)
                for d in range(HALF):
                    mm = conv_lag(j, 0, d)
                mm.then_inc(conv_done, 1)
                for d in range(NC):
                    mm = conv_lag(j, 1, d)
                    if middle is not None and d == 3:
                        middle()
                mm.then_inc(conv_done, 1)

            def linear(i):
                for c in range(NC):
                    if c % HALF == 0:
                        pe.wait_ge(y_hi_ready, 2 * i + c // HALF + 1)
                        pe.wait_ge(y_lo_ready, 2 * i + c // HALF + 1)
                    for n, (y, w) in enumerate(((y_hi, w_hi), (y_hi, w_lo), (y_lo, w_hi))):
                        for s in range(3):
                            mm = pe.matmul(ps_base[s][:, 0:SEG[s + 1] - SEG[s]], y[:, c, :],
                                           w[:, c, SEG[s]:SEG[s + 1]], start=(c == 0 and n == 0),
                                           stop=(c == NC - 1 and n == 2))
                mm.then_inc(base_done, 1)

            def turn_hw(i):
                pe.wait_ge(hw_ready, i + 1)
                pe.transpose(ps_h[:, 0:P], hw[:].rearrange("p e r -> p (e r)"), ident[:]).then_inc(hw_turned, 1)

            def lora(i):
                pe.wait_ge(hwt_hi_ready, i + 1)
                pe.wait_ge(hwt_lo_ready, i + 1)
                for s in range(3):
                    a, b = LSEG[s], LSEG[s + 1]
                    for n, (h, w) in enumerate(((hwt_hi, b2_hi), (hwt_hi, b2_lo), (hwt_lo, b2_hi))):
                        mm = pe.matmul(ps_base[s][:, 0:b - a], h[:], w[:, a:b], start=False, stop=(n == 2),
                                       skip_group_check=True)
                    mm.then_inc(lora_done, 1)

            turn_x(0)
            conv(0, 0, 16)
            turn_x(1)
            with pe.Fori(0, H // UNROLL - 1) as t:
                for j in range(UNROLL):
                    i = UNROLL * t + j
                    linear(i)
                    conv(i + 1, j + 1, 32 * t + 16 * ((j + 1) // TS + 1), middle=lambda: turn_hw(i))
                    lora(i)
                    turn_x(i + 2)
                    for s in range(3):
                        pe.wait_ge(out_ready[s], i + 1)
            for i in range(H - UNROLL, H):
                linear(i)
                if i + 1 < H:
                    conv(i + 1, i + 1, 16 * ((i + 1) // TS + 1), middle=lambda: turn_hw(i))
                else:
                    turn_hw(i)
                lora(i)
                if i + 2 < H:
                    turn_x(i + 2)
                if i + 1 < H:
                    for s in range(3):
                        pe.wait_ge(out_ready[s], i + 1)


_INS = ['x', 'itok_B_8_3872', 'L0_cond_log_dt', 'L0_cond_C', 'L0_cond_log_A_real', 'L0_cond_A_imag', 'L0_cond_D',
        'L0_ffn_W_base', 'L0_ffn_b_base', 'L0_ffn_W_router', 'L0_ffn_A', 'L0_ffn_B']


def kernel(**inputs):
    import concourse.bacc as _bacc
    from concourse.bass_utils import run_bass_kernel_spmd as _run

    nc = _bacc.Bacc("TRN2", target_bir_lowering=False, num_devices=1)
    arrays, args = {}, []
    for name in _INS:
        a = np.ascontiguousarray(inputs[name])
        arrays[f"in_{name}_dram"] = a
        args.append(nc.dram_tensor(f"in_{name}_dram", a.shape, mybir.dt.from_np(a.dtype), kind="ExternalInput").ap())
    args.append(nc.dram_tensor("out_0_dram", inputs['x'].shape, F32, kind="ExternalOutput").ap())
    s4d_lora_ffn(nc, *args)
    r = _run(nc, [arrays], core_ids=[0])
    return r.results[0]["out_0_dram"]
```

```python
from contextlib import ExitStack
import math

import numpy as np
import concourse.bass as bass
from concourse import mybir

F32 = mybir.dt.float32
F32R = mybir.dt.float32r
I32 = mybir.dt.int32
AX_X = mybir.AxisListType.X
ALU = mybir.AluOpType
ACT = mybir.ActivationFunctionType

P = 128
BANK = 512
MAGIC = 1.5 * 2.0 ** 23
LOG2E = 1.0 / math.log(2.0)
LN2_HI = 0.693359375
LN2_LO = math.log(2.0) - LN2_HI
TWO_PI_1 = 6.28125
TWO_PI_2 = math.floor((2 * math.pi - TWO_PI_1) * 2.0 ** 20) / 2.0 ** 20
TWO_PI_3 = 2 * math.pi - TWO_PI_1 - TWO_PI_2
PI_BELOW = 3.1415925


def s4d_lora_ffn(nc, x, lengths, log_dt, C, log_A_real, A_imag, D, W_base, b_base, W_router, A_lora, B_lora, out):
    B, H, L = x.shape
    N = A_imag.shape[1]
    E, R, _ = A_lora.shape
    O = W_base.shape[0]
    ER = E * R
    NC = L // P
    HALF = NC // 2
    HC = HALF * P
    assert B == P and ER == P and 2 * N == P and HC == BANK and O == L and H % 4 == 0
    SCALING = 32.0 / R
    COLS = O + ER + E
    SEG = [0, 388, 776, COLS]
    LSEG = [0, 388, 776, O]
    A0, R0 = O - SEG[2], O + ER - SEG[2]
    HP = H // 2
    NV = NC - 1
    UNROLL = 4
    GP = UNROLL // 2
    NPOS = P + 1
    LAM_RE, FCOL, LAM_IM = P, NPOS, 2 * NPOS
    TROW = 2 * NPOS + 2
    KROW = 2 * P
    ROUTE_STEPS, GEN_STEPS, TAB_STEPS, KSUM_STEPS = 10, 6, 6, 2
    STATE_STEPS = 2 * (NV - 1)
    ANGLE_STEPS, K_STEPS = 9, 4
    ANGLES_AT = ((), (0, 1), (2,), (3,), (4,), (5,), (6, 7))
    K_AT = ((), (), (), (0,), (1,), (2,), (3,))

    tab_dram = nc.dram_tensor("tab_dram", [H, P, TROW], F32, kind="Internal")
    k_dram = nc.dram_tensor("k_dram", [H, 2, KROW], F32, kind="Internal")

    with ExitStack() as ctx:
        def sb(name, shape, dt=F32):
            return ctx.enter_context(nc.sbuf_tensor(name, shape, dt))

        def sem(name):
            return ctx.enter_context(nc.semaphore(name))

        w_hi = sb("w_hi", [P, NC, COLS], F32R)
        w_lo = sb("w_lo", [P, NC, COLS], F32R)
        b2_hi = sb("b2_hi", [P, O], F32R)
        b2_lo = sb("b2_lo", [P, O], F32R)
        bias_rows = sb("bias_rows", [P, O])
        mask_rows = sb("mask_rows", [P, L])
        mask_cols = sb("mask_cols", [P, NC, P])
        ident = sb("ident", [P, P])
        lower = sb("lower", [P, E, E])
        rank_limit = sb("rank_limit", [P, E])
        half_pi = sb("half_pi", [P, 1])
        pos = sb("pos", [P, NPOS])
        parity = sb("parity", [P, 2])
        signs = sb("signs", [P, 2, GP])
        coef = sb("coef", [P, 5, HP])
        d_rows = sb("d_rows", [2, HP])
        x_slot = sb("x_slot", [P, UNROLL, L])
        xm = sb("xm", [P, L])
        u_hi = sb("u_hi", [P, 2, NC, P], F32R)
        u_lo = sb("u_lo", [P, 2, NC, P], F32R)
        ym = sb("ym", [P, NC, P])
        y_hi = sb("y_hi", [P, NC, P], F32R)
        y_lo = sb("y_lo", [P, NC, P], F32R)
        tab = sb("tab", [P, UNROLL, TROW])
        toep = sb("toep", [P, UNROLL, 2, P], F32R)
        g_hi = sb("g_hi", [P, P], F32R)
        g_lo = sb("g_lo", [P, P], F32R)
        f_hi = sb("f_hi", [P, 2, P], F32R)
        f_lo = sb("f_lo", [P, 2, P], F32R)
        state = sb("state", [P, NV, P])
        cross = sb("cross", [P, P])
        s_hi = sb("s_hi", [P, NV, P], F32R)
        s_lo = sb("s_lo", [P, NV, P], F32R)
        logit = sb("logit", [P, E])
        top = sb("top", [P, 1])
        below = sb("below", [P, E])
        weight = sb("weight", [P, E])
        before = sb("before", [P, E, E])
        balance = sb("balance", [P, E, E])
        rank = sb("rank", [P, E])
        gate = sb("gate", [P, E])
        total = sb("total", [P, 1])
        hw = sb("hw", [P, E, R])
        hwt_hi = sb("hwt_hi", [P, P], F32R)
        hwt_lo = sb("hwt_lo", [P, P], F32R)
        cur = sb("cur", [P, 5, GP])
        theta = sb("theta", [P, GP, NPOS])
        turns = sb("turns", [P, GP, NPOS])
        decay = sb("decay", [P, GP, NPOS])
        sines = sb("sines", [P, GP, NPOS])
        cosines = sb("cosines", [P, GP, NPOS])
        term_a = sb("term_a", [P, GP, NPOS])
        term_b = sb("term_b", [P, GP, NPOS])
        comb = sb("comb", [P, 2, GP, TROW])
        k_full = sb("k_full", [2, GP, P])
        k_split = sb("k_split", [2, 2, GP, P], F32R)
        stage = sb("stage", [P, 4, L])
        nat = sb("nat", [N, 5, 2, N])
        lin = sb("lin", [H, N + 1])
        aim = sb("aim", [H, N])
        cc = sb("cc", [H, N, 2])
        small = [sb(f"small{i}", [H, N + 1]) for i in range(9)]
        ki = sb("ki", [H, N + 1], I32)
        len_col = sb("len_col", [P, 1], I32)
        len_colf = sb("len_colf", [P, 1])
        len_row = sb("len_row", [P, P], I32)
        len_rowf = sb("len_rowf", [P, P])
        chunk_pos = sb("chunk_pos", [P, NC])
        zeros = state[0:H, 0:2, :]
        router_stage = ym[0:E, :, :].rearrange("e c n -> e (c n)")

        def bank(name):
            return ctx.enter_context(nc.psum_tensor(name, [P, BANK], F32))

        ps_base = [bank(f"ps_base{s}") for s in range(3)]
        ps_y = [bank(f"ps_y{s}") for s in range(2)]
        ps_u = [bank(f"ps_u{s}") for s in range(2)]
        ps_h = bank("ps_h")
        k_bank = ps_h[0:2, P:P + GP * P]

        params_in = sem("params_in")
        lens_in = sem("lens_in")
        bias_in = sem("bias_in")
        d_in = sem("d_in")
        stage_in = [sem(f"stage_in{i}") for i in range(4)]
        router_in = sem("router_in")
        const_ready = sem("const_ready")
        zeros_ready = sem("zeros_ready")
        lens_float = sem("lens_float")
        masks_ready = sem("masks_ready")
        pool_chain = sem("pool_chain")
        dve_chain = sem("dve_chain")
        half_angle = sem("half_angle")
        half_sin = sem("half_sin")
        nat_ready = sem("nat_ready")
        nat_turned = sem("nat_turned")
        coef_ready = sem("coef_ready")
        pad_stored = sem("pad_stored")
        wt_turned = sem("wt_turned")
        wt_hi_ready = sem("wt_hi_ready")
        wt_lo_ready = sem("wt_lo_ready")
        cur_ready = sem("cur_ready")
        gen_chain = sem("gen_chain")
        angle_ready = sem("angle_ready")
        decay_arg = sem("decay_arg")
        sincos_ready = sem("sincos_ready")
        tab_chain = sem("tab_chain")
        comb_ready = sem("comb_ready")
        tab_stored = sem("tab_stored")
        k_summed = sem("k_summed")
        ksum_chain = sem("ksum_chain")
        k_ready = sem("k_ready")
        k_stored = sem("k_stored")
        x_loaded = [sem(f"x_loaded{i}") for i in range(UNROLL)]
        tab_loaded = [sem(f"tab_loaded{i}") for i in range(UNROLL)]
        toep_loaded = [sem(f"toep_loaded{i}") for i in range(UNROLL)]
        stored = [sem(f"stored{i}") for i in range(UNROLL)]
        x_masked = sem("x_masked")
        x_biased = sem("x_biased")
        u_turned = sem("u_turned")
        u_hi_ready = sem("u_hi_ready")
        u_lo_ready = sem("u_lo_ready")
        g_turned = sem("g_turned")
        gf_hi_ready = sem("gf_hi_ready")
        gf_lo_ready = sem("gf_lo_ready")
        v_done = sem("v_done")
        v_copied = sem("v_copied")
        cross_ready = sem("cross_ready")
        state_chain = sem("state_chain")
        s_hi_ready = sem("s_hi_ready")
        s_lo_ready = sem("s_lo_ready")
        conv_done = sem("conv_done")
        y_masked = sem("y_masked")
        y_hi_ready = sem("y_hi_ready")
        y_lo_ready = sem("y_lo_ready")
        h_done = sem("h_done")
        below_ready = sem("below_ready")
        weight_ready = sem("weight_ready")
        route_chain = sem("route_chain")
        hw_ready = sem("hw_ready")
        hw_turned = sem("hw_turned")
        hwt_hi_ready = sem("hwt_hi_ready")
        hwt_lo_ready = sem("hwt_lo_ready")
        lora_done = sem("lora_done")
        out_ready = [sem(f"out_ready{s}") for s in range(3)]

        NB = O // P
        blocks = [(W_base[P * i:P * (i + 1), :], P * i) for i in range(NB)]
        blocks.append((A_lora.rearrange("e r d -> (e r) d"), O))
        units = [(i, col, c0) for i, (_, col) in enumerate(blocks) for c0 in (0, HALF)]
        B_UNIT = len(units)
        NUNITS = B_UNIT + 3
        b_slot = len(blocks) % 4
        unit_bank = [ps_base[0], ps_base[1], ps_base[2], ps_y[1]]
        UNITS_1, UNITS_2 = 4, 14

        def weight_unit(pe, u):
            if u >= 4:
                pe.wait_ge(wt_lo_ready, u - 3)
            dst = unit_bank[u % 4]
            if u < B_UNIT:
                blk, _, c0 = units[u]
                pe.wait_ge(stage_in[blk % 4], 16 * (blk // 4 + 1))
                for k in range(HALF):
                    mm = pe.transpose(dst[:, k * P:(k + 1) * P], stage[:, blk % 4, (c0 + k) * P:(c0 + k + 1) * P],
                                      ident[:])
            elif u < B_UNIT + 2:
                pe.wait_ge(stage_in[b_slot], 16 * (len(blocks) // 4) + 16 * E)
                for k in range(HALF):
                    c = (u - B_UNIT) * HALF + k
                    mm = pe.transpose(dst[:, k * P:(k + 1) * P], stage[:, b_slot, c * P:(c + 1) * P], ident[:])
            else:
                pe.wait_ge(router_in, 16)
                for c in range(NC):
                    mm = pe.transpose(dst[:, c * E:(c + 1) * E], router_stage[:, c * P:(c + 1) * P], ident[0:E, 0:E])
            mm.then_inc(wt_turned, 1)

        def unit_views(u):
            src = unit_bank[u % 4]
            if u < B_UNIT:
                _, col, c0 = units[u]
                return (src[:].rearrange("p (c n) -> p c n", c=HALF), w_hi[:, c0:c0 + HALF, col:col + P],
                        w_lo[:, c0:c0 + HALF, col:col + P], 1.0)
            if u < B_UNIT + 2:
                at = (u - B_UNIT) * HC
                return src[:], b2_hi[:, at:at + HC], b2_lo[:, at:at + HC], SCALING
            return (src[:, 0:NC * E].rearrange("p (c n) -> p c n", c=NC), w_hi[:, :, O + ER:COLS],
                    w_lo[:, :, O + ER:COLS], 1.0)

        def tab_source(h):
            return tab_dram[h, :, 0:TROW - 1]

        def toeplitz_source(h):
            return bass.AP(k_dram, h * (2 * KROW) + 1, [[1, P], [KROW, 2], [1, P]])

        def i_left(i, ahead):
            return not isinstance(i, int) or i + ahead < H

        xm_reversed = bass.AP(xm, P - 1, [[L, P], [P, NC], [-1, P]])
        chunked = "p (c n) -> p c n"
        block = ctx.enter_context(nc.Block())

        @block.sync
        def _(sp):
            def load_tab(h, j):
                sp.dma_start(tab[:, j, 0:TROW - 1], tab_source(h)).then_inc(tab_loaded[j], 16)

            def load_toep(h, j):
                sp.dma_start(toep[:, j, :, :].bitcast(F32), toeplitz_source(h)).then_inc(toep_loaded[j], 16)

            def store_tables(g):
                sp.wait_ge(comb_ready, g + 1)
                for par in range(2):
                    for half in range(2):
                        dst = bass.AP(tab_dram, (g * UNROLL + par) * (P * TROW) + half * N * TROW,
                                      [[TROW, N], [2 * P * TROW, GP], [1, TROW - 1]])
                        sp.dma_start(dst, comb[N * par:N * (par + 1), half, :, 0:TROW - 1]).then_inc(tab_stored, 16)
                sp.wait_ge(tab_stored, 64 * g + 64)

            def store_k(g):
                sp.wait_ge(k_ready, 2 * g + 2)
                for part in range(2):
                    dst = bass.AP(k_dram, (g * UNROLL) * (2 * KROW) + part * KROW + P,
                                  [[2 * KROW, 2], [4 * KROW, GP], [1, P]])
                    sp.dma_start(dst, k_split[:, part, :, :].bitcast(F32)).then_inc(k_stored, 16)
                sp.wait_ge(k_stored, 32 * g + 32)

            sp.dma_start(lin[:, 0:N], log_A_real).then_inc(params_in, 16)
            sp.dma_start(lin[:, N:N + 1], log_dt.rearrange("(h o) -> h o", o=1)).then_inc(params_in, 16)
            sp.dma_start(aim[:], A_imag).then_inc(params_in, 16)
            sp.dma_start(cc[:], C).then_inc(params_in, 16)
            sp.dma_start(len_col[:], lengths.rearrange("(b o) -> b o", o=1)).then_inc(lens_in, 16)
            sp.dma_start(len_row[:], bass.AP(lengths.tensor, 0, [[0, P], [1, B]])).then_inc(lens_in, 16)
            for i in range(4):
                sp.dma_start(stage[:, i, :], blocks[i][0]).then_inc(stage_in[i], 16)
            sp.dma_start(x_slot[:, 0, :], x[:, 0, :]).then_inc(x_loaded[0], 16)
            with nc.allow_non_contiguous_dma(reason="64 values, once"):
                sp.dma_start(d_rows[:], D.rearrange("(g two) -> two g", two=2)).then_inc(d_in, 16)
            sp.dma_start(router_stage, W_router).then_inc(router_in, 16)
            sp.dma_start(bias_rows[:], bass.AP(b_base.tensor, 0, [[0, P], [1, O]])).then_inc(bias_in, 16)
            sp.wait_ge(zeros_ready, 1)
            sp.dma_start(bass.AP(k_dram, 0, [[2 * KROW, H], [KROW, 2], [1, P]]), zeros).then_inc(pad_stored, 16)

            def next_block(i):
                sp.wait_ge(wt_turned, 2 * (i - 4) + 2)
                if i < len(blocks):
                    sp.dma_start(stage[:, i % 4, :], blocks[i][0]).then_inc(stage_in[i % 4], 16)
                else:
                    for e in range(E):
                        dst = stage[:, b_slot, :].rearrange("p (c e r) -> p c e r", c=NB, e=E)[:, :, e, :]
                        sp.dma_start(dst, B_lora[e].rearrange("(c p) r -> p c r", p=P)).then_inc(stage_in[b_slot], 16)

            for i in range(4, 6):
                next_block(i)
            store_tables(0)
            for h in range(UNROLL - 1):
                load_tab(h, h)
            for i in range(6, 8):
                next_block(i)
            for h in range(1, UNROLL):
                sp.dma_start(x_slot[:, h, :], x[:, h, :]).then_inc(x_loaded[h], 16)
            sp.wait_ge(pad_stored, 16)
            store_k(0)
            for h in range(2):
                load_toep(h, h)
            for i in range(8, len(blocks) + 1):
                next_block(i)

            def head(i, j, g=None, last=False):
                if j == 1 and not last:
                    store_tables(g)
                if not last or j + 3 < UNROLL:
                    load_tab(i + 3, (j + 3) % UNROLL)
                if j == 2 and not last:
                    store_k(g)
                if not last or j + 2 < UNROLL:
                    load_toep(i + 2, (j + 2) % UNROLL)
                for s in range(3):
                    sp.wait_ge(out_ready[s], i + 1)
                sp.dma_start(out[:, i, :], x_slot[:, j, :]).then_inc(stored[j], 16)

            with sp.Fori(0, H // UNROLL - 1) as t:
                for j in range(UNROLL):
                    i = UNROLL * t + j
                    head(i, j, t + 1)
                    sp.wait_ge(stored[j], 16 * t + 16)
                    sp.dma_start(x_slot[:, j, :], x[:, i + UNROLL, :]).then_inc(x_loaded[j], 16)
            for j in range(UNROLL):
                head(H - UNROLL + j, j, last=True)
            for j in range(UNROLL):
                sp.wait_ge(stored[j], 16 * (H // UNROLL))

        @block.gpsimd
        def _(pool):
            count = [0]

            def link(ins):
                count[0] += 1
                ins.then_inc(pool_chain, 1)
                pool.wait_ge(pool_chain, count[0])

            def iota(dst, pattern, base=0, channel=0):
                return pool.iota(dst, pattern, base=base, channel_multiplier=channel,
                                 allow_small_or_imprecise_dtypes=True)

            link(pool.memset(ident[:], 0.0))
            pool.affine_select(out=ident[:], in_=ident[:], compare_op=ALU.not_equal, fill=1.0, base=0,
                               pattern=[[-1, P]], channel_multiplier=1).then_inc(const_ready, 1)
            pool.memset(half_pi[:], math.pi / 2).then_inc(const_ready, 1)
            iota(pos[:], [[1, NPOS]]).then_inc(const_ready, 1)
            link(pool.memset(parity[:], 0.0))
            pool.memset(signs[:, 0, :], 1.0)
            pool.memset(signs[:, 1, :], -1.0)
            iota(rank_limit[:], [[1, E]], base=3 - E).then_inc(const_ready, 1)
            link(pool.memset(lower[:], 1.0))
            pool.affine_select(out=lower[:], in_=lower[:], compare_op=ALU.is_gt, fill=0.0, base=0,
                               pattern=[[1, E], [-1, E]], channel_multiplier=0).then_inc(const_ready, 1)
            pool.wait_ge(const_ready, 5)
            link(pool.memset(parity[0:N, 0:1], 1.0))
            pool.memset(parity[N:P, 1:2], 1.0).then_inc(const_ready, 1)
            pool.wait_ge(const_ready, 6)
            pool.memset(zeros, 0.0).then_inc(zeros_ready, 1)
            iota(chunk_pos[:], [[P, NC]], channel=1)
            link(iota(mask_rows[:], [[1, L]]))
            pool.wait_ge(lens_float, 2)
            link(pool.tensor_scalar(mask_rows[:], mask_rows[:], len_colf[:, 0:1], None, ALU.is_lt))
            for c in range(NC):
                ins = pool.tensor_scalar(mask_cols[:, c, :], len_rowf[:], chunk_pos[:, c:c + 1], None, ALU.is_gt)
                ins.then_inc(masks_ready, 1)

            def mask_x(i, j, loads):
                pool.wait_ge(x_loaded[j], loads)
                pool.tensor_tensor(xm_reversed, x_slot[:, j, :].rearrange(chunked, c=NC),
                                   mask_rows[:].rearrange(chunked, c=NC), ALU.mult).then_inc(x_masked, 1)
                pool.wait_ge(x_masked, i + 1)
                pool.tensor_tensor(x_slot[:, j, :], x_slot[:, j, :], bias_rows[:], ALU.add).then_inc(x_biased, 1)

            def over_pairs(q):
                return cur[:, q, :].unsqueeze(2).broadcast_to([P, GP, NPOS])

            def decay_argument(g):
                pool.wait_ge(cur_ready, g + 1)
                pool.tensor_tensor(decay[:], over_pairs(0), pos[:].unsqueeze(1).broadcast_to([P, GP, NPOS]),
                                   ALU.mult).then_inc(decay_arg, 1)

            def tables(g, first=False):
                done = [0]

                def then(ins):
                    done[0] += 1
                    ins.then_inc(tab_chain, 1)
                    pool.wait_ge(tab_chain, TAB_STEPS * g + done[0])

                if not first:
                    pool.wait_ge(tab_stored, 64 * g)
                    pool.wait_ge(k_summed, g)
                pool.wait_ge(sincos_ready, 3 * g + 3)
                e_re, e_im = comb[:, 0, :, 0:NPOS], comb[:, 1, :, 0:NPOS]
                f_re, f_im = comb[:, 0, :, FCOL:FCOL + NPOS], comb[:, 1, :, FCOL:FCOL + NPOS]
                pool.tensor_tensor(e_im, decay[:], sines[:], ALU.mult)
                then(pool.tensor_tensor(e_re, decay[:], cosines[:], ALU.mult))
                pool.tensor_tensor(term_a[:], e_re, over_pairs(2), ALU.mult)
                then(pool.tensor_tensor(term_b[:], e_im, over_pairs(3), ALU.mult))
                then(pool.tensor_tensor(f_re, term_a[:], term_b[:], ALU.subtract))
                pool.tensor_tensor(term_a[:], e_im, over_pairs(4), ALU.mult)
                then(pool.tensor_tensor(term_b[:], e_re, over_pairs(3), ALU.mult))
                then(pool.tensor_tensor(f_im, term_a[:], term_b[:], ALU.subtract))
                then(pool.tensor_tensor(comb[:, :, :, LAM_IM], comb[:, 1, :, P].unsqueeze(1).broadcast_to([P, 2, GP]),
                                        signs[:], ALU.mult))
                assert done[0] == TAB_STEPS
                pool.tensor_tensor(comb[:, 1, :, LAM_RE], comb[:, 0, :, LAM_RE], signs[:, 0, :],
                                   ALU.mult).then_inc(comb_ready, 1)

            pool.wait_ge(const_ready, 6)
            decay_argument(0)
            tables(0, first=True)
            pool.wait_ge(bias_in, 16)
            mask_x(0, 0, 16)
            for h in (1, 2):
                pool.wait_ge(u_turned, 2 * h)
                mask_x(h, h, 16)
            with pool.Fori(0, H // UNROLL - 1) as t:
                for j in range(UNROLL):
                    i = UNROLL * t + j
                    if j == 0:
                        decay_argument(t + 1)
                    pool.wait_ge(u_turned, 2 * i + 6)
                    mask_x(i + 3, (j + 3) % UNROLL, 16 * t + 16 + 16 * ((j + 3) // UNROLL))
                    if j == 0:
                        tables(t + 1)
            i = H - UNROLL
            pool.wait_ge(u_turned, 2 * i + 6)
            mask_x(i + 3, UNROLL - 1, 16 * (H // UNROLL))

        @block.scalar
        def _(act):
            def weight_high(u):
                act.wait_ge(wt_turned, u + 1)
                src, hi, _, factor = unit_views(u)
                act.activation(hi, src, ACT.Copy, scale=factor).then_inc(wt_hi_ready, 1)

            def group_decay(g):
                act.wait_ge(decay_arg, g + 1)
                act.activation(decay[:], decay[:], ACT.Exp).then_inc(sincos_ready, 1)

            def group_sincos(g):
                act.wait_ge(angle_ready, 2 * g + 1)
                act.activation(sines[:], theta[:], ACT.Sin).then_inc(sincos_ready, 1)
                act.wait_ge(angle_ready, 2 * g + 2)
                act.activation(cosines[:], turns[:], ACT.Sin, scale=-1.0, bias=half_pi[:]).then_inc(sincos_ready, 1)

            def split_u(i, j):
                for half in range(2):
                    act.wait_ge(u_turned, 2 * i + half + 1)
                    c = slice(half * HALF, (half + 1) * HALF)
                    act.activation(u_hi[:, j % 2, c, :], ps_u[half][:].rearrange(chunked, c=HALF),
                                   ACT.Copy).then_inc(u_hi_ready, 1)

            def split_gf(i, j):
                act.wait_ge(g_turned, i + 1)
                act.activation(g_hi[:], ps_h[:, 0:P], ACT.Copy).then_inc(gf_hi_ready, 1)
                act.activation(f_hi[:, j % 2, :], tab[:, j % UNROLL, FCOL + 1:FCOL + NPOS],
                               ACT.Copy).then_inc(gf_hi_ready, 1)

            def copy_v(i):
                act.wait_ge(v_done, i + 1)
                act.activation(state[:, 0:HALF, :], ps_u[0][:].rearrange(chunked, c=HALF), ACT.Copy)
                act.activation(state[:, HALF:NV, :], ps_u[1][:, 0:(NV - HALF) * P].rearrange(chunked, c=NV - HALF),
                               ACT.Copy).then_inc(v_copied, 1)

            def cross_terms(i, j, c):
                if c == 1:
                    act.wait_ge(v_copied, i + 1)
                else:
                    act.wait_ge(state_chain, STATE_STEPS * i + 2 * (c - 1))
                lam = tab[:, j % UNROLL, LAM_IM:LAM_IM + 1]
                act.activation(cross[0:N, :], state[N:P, c - 1, :], ACT.Copy, scale=lam[N:P])
                act.activation(cross[N:P, :], state[0:N, c - 1, :], ACT.Copy, scale=lam[0:N]).then_inc(cross_ready, 1)

            def split_state(i, half):
                a, b = (0, HALF - 1) if half == 0 else (HALF - 1, NV)
                act.wait_ge(state_chain, STATE_STEPS * i + 2 * (b - 1))
                act.activation(s_hi[:, a:b, :], state[:, a:b, :], ACT.Copy).then_inc(s_hi_ready, 1)

            def states(i, j, half):
                for c in ((1, 2) if half == 0 else range(3, NV)):
                    cross_terms(i, j, c)
                split_state(i, half)

            def split_y(i, half):
                act.wait_ge(y_masked, 2 * i + half + 1)
                c = slice(half * HALF, (half + 1) * HALF)
                act.activation(y_hi[:, c, :], ym[:, c, :], ACT.Copy).then_inc(y_hi_ready, 1)

            for u in range(UNITS_1):
                weight_high(u)
            act.wait_ge(const_ready, 2)
            act.wait_ge(half_angle, 1)
            act.activation(small[4][:, 0:N], small[2][:, 0:N], ACT.Sin, scale=0.5).then_inc(half_sin, 1)
            act.activation(small[5][:, 0:N], small[3][:, 0:N], ACT.Sin, scale=-0.5,
                           bias=half_pi[0:H, :]).then_inc(half_sin, 1)
            group_sincos(0)
            group_decay(0)
            for u in range(UNITS_1, UNITS_2):
                weight_high(u)
            split_u(0, 0)
            act.wait_ge(tab_loaded[0], 16)
            split_gf(0, 0)
            act.wait_ge(pad_stored, 16)
            copy_v(0)
            states(0, 0, 0)
            states(0, 0, 1)
            for u in range(UNITS_2, NUNITS):
                weight_high(u)
            split_u(1, 1)
            act.wait_ge(tab_loaded[1], 16)
            split_gf(1, 1)
            split_y(0, 0)
            split_y(0, 1)
            copy_v(1)

            act.wait_ge(conv_done, 2)
            split_u(2, 2)
            act.wait_ge(tab_loaded[2], 16)
            split_gf(2, 2)

            def head(i, j, t=None):
                if i_left(i, 1):
                    states(i + 1, j + 1, 0)
                    states(i + 1, j + 1, 1)
                act.wait_ge(below_ready, i + 1)
                act.activation(weight[:], below[:], ACT.Exp).then_inc(weight_ready, 1)
                if j == 0 and t is not None:
                    group_decay(t + 1)
                if i_left(i, 2):
                    act.wait_ge(s_lo_ready, 2 * i + 4)
                    copy_v(i + 2)
                if j == 0 and t is not None:
                    group_sincos(t + 1)
                act.wait_ge(hw_turned, i + 1)
                act.activation(hwt_hi[:], ps_h[:, 0:P], ACT.Copy).then_inc(hwt_hi_ready, 1)
                if i_left(i, 1):
                    split_y(i + 1, 0)
                    split_y(i + 1, 1)
                if i_left(i, 3):
                    act.wait_ge(conv_done, 2 * i + 4)
                    split_u(i + 3, j + 3)
                    loads = 16 * (H // UNROLL) if t is None else 16 * t + 16 + 16 * ((j + 3) // UNROLL)
                    act.wait_ge(tab_loaded[(j + 3) % UNROLL], loads)
                    split_gf(i + 3, j + 3)

            with act.Fori(0, H // UNROLL - 1) as t:
                for j in range(UNROLL):
                    head(UNROLL * t + j, j, t)
            for i in range(H - UNROLL, H):
                head(i, i % UNROLL)

        @block.vector
        def _(dve):
            count = [0]

            def link(ins):
                count[0] += 1
                ins.then_inc(dve_chain, 1)
                dve.wait_ge(dve_chain, count[0])

            def ts(o, i, s1, s2, op0, op1):
                link(dve.tensor_scalar(o, i, s1, s2, op0, op1))

            def tt(o, a, b, op):
                link(dve.tensor_tensor(o, a, b, op))

            def stt(o, a, s, b, op0, op1):
                link(dve.scalar_tensor_tensor(out=o, in0=a, scalar=s, in1=b, op0=op0, op1=op1))

            def exponential(v, n, e_out, em1_out, k, r, p):
                ts(r, v, -87.0, 88.0, ALU.max, ALU.min)
                ts(k, r, LOG2E, MAGIC, ALU.mult, ALU.add)
                ts(k, k, -MAGIC, None, ALU.add, ALU.bypass)
                stt(r, k, -LN2_HI, r, ALU.mult, ALU.add)
                stt(r, k, -LN2_LO, r, ALU.mult, ALU.add)
                ts(p, r, 1.0 / 5040, None, ALU.mult, ALU.bypass)
                for f in (720, 120, 24, 6, 2, 1):
                    stt(p, p, 1.0 / f, r, ALU.add, ALU.mult)
                ts(ki[:, 0:n], k, 127.0, 2.0 ** 23, ALU.add, ALU.mult)
                pow2 = ki[:, 0:n].bitcast(F32)
                tt(p, p, pow2, ALU.mult)
                if e_out is not None:
                    tt(e_out, p, pow2, ALU.add)
                if em1_out is not None:
                    stt(em1_out, pow2, -1.0, p, ALU.add, ALU.add)

            def reduce_angle(then, r, q):
                then(dve.tensor_scalar(q, r, 1 / (2 * math.pi), MAGIC, ALU.mult, ALU.add))
                then(dve.tensor_scalar(q, q, -MAGIC, None, ALU.add, ALU.bypass))
                for part in (TWO_PI_1, TWO_PI_2, TWO_PI_3):
                    then(dve.scalar_tensor_tensor(out=r, in0=q, scalar=-part, in1=r, op0=ALU.mult, op1=ALU.add))

            def magnitude(dst, src):
                return dve.scalar_tensor_tensor(out=dst, in0=src, scalar=-1.0, in1=src, op0=ALU.mult, op1=ALU.max)

            def angle_step(g, n, first=False):
                wide = [P, GP, NPOS]
                if 1 < n < 8:
                    dve.wait_ge(gen_chain, GEN_STEPS * g + n - 1)
                if n == 0:
                    if not first:
                        dve.wait_ge(comb_ready, g)
                    dve.tensor_copy(cur[:], coef[:, :, bass.ds(GP * g, GP)]).then_inc(cur_ready, 1)
                elif n == 1:
                    dve.wait_ge(cur_ready, g + 1)
                    dve.tensor_tensor(theta[:], cur[:, 1, :].unsqueeze(2).broadcast_to(wide),
                                      pos[:].unsqueeze(1).broadcast_to(wide), ALU.mult).then_inc(gen_chain, 1)
                elif n == 2:
                    dve.tensor_scalar(turns[:], theta[:], 1 / (2 * math.pi), MAGIC, ALU.mult,
                                      ALU.add).then_inc(gen_chain, 1)
                elif n == 3:
                    dve.tensor_scalar(turns[:], turns[:], -MAGIC, None, ALU.add, ALU.bypass).then_inc(gen_chain, 1)
                elif n < 7:
                    part = (TWO_PI_1, TWO_PI_2, TWO_PI_3)[n - 4]
                    dve.scalar_tensor_tensor(out=theta[:], in0=turns[:], scalar=-part, in1=theta[:], op0=ALU.mult,
                                             op1=ALU.add).then_inc(gen_chain, 1)
                elif n == 7:
                    dve.tensor_scalar(theta[:], theta[:], -PI_BELOW, PI_BELOW, ALU.max,
                                      ALU.min).then_inc(angle_ready, 1)
                else:
                    dve.wait_ge(angle_ready, 2 * g + 1)
                    magnitude(turns[:], theta[:]).then_inc(angle_ready, 1)

            def k_step(g, n):
                if n == 0:
                    dve.wait_ge(k_summed, g + 1)
                    dve.tensor_copy(k_full[:], k_bank.rearrange(chunked, c=GP)).then_inc(ksum_chain, 1)
                elif n == 1:
                    dve.wait_ge(ksum_chain, KSUM_STEPS * g + 1)
                    dve.tensor_tensor(k_full[:, :, 0], k_full[:, :, 0], d_rows[:, bass.ds(GP * g, GP)],
                                      ALU.add).then_inc(ksum_chain, 1)
                elif n == 2:
                    dve.wait_ge(ksum_chain, KSUM_STEPS * g + 2)
                    dve.tensor_copy(k_split[:, 0, :, :], k_full[:]).then_inc(k_ready, 1)
                else:
                    dve.wait_ge(k_ready, 2 * g + 1)
                    dve.tensor_tensor(k_split[:, 1, :, :], k_full[:], k_split[:, 0, :, :].bitcast(F32),
                                      ALU.subtract).then_inc(k_ready, 1)

            def weight_low(u):
                dve.wait_ge(wt_hi_ready, u + 1)
                src, hi, lo, factor = unit_views(u)
                dve.scalar_tensor_tensor(out=lo, in0=src, scalar=factor, in1=hi.bitcast(F32),
                                         op0=ALU.mult, op1=ALU.subtract).then_inc(wt_lo_ready, 1)

            def split_u(i, j):
                for half in range(2):
                    dve.wait_ge(u_hi_ready, 2 * i + half + 1)
                    c = slice(half * HALF, (half + 1) * HALF)
                    dve.tensor_tensor(u_lo[:, j % 2, c, :], ps_u[half][:].rearrange(chunked, c=HALF),
                                      u_hi[:, j % 2, c, :].bitcast(F32), ALU.subtract).then_inc(u_lo_ready, 1)

            def split_gf(i, j):
                dve.wait_ge(gf_hi_ready, 2 * i + 2)
                dve.tensor_tensor(g_lo[:], ps_h[:, 0:P], g_hi[:].bitcast(F32), ALU.subtract).then_inc(gf_lo_ready, 1)
                dve.tensor_tensor(f_lo[:, j % 2, :], tab[:, j % UNROLL, FCOL + 1:FCOL + NPOS],
                                  f_hi[:, j % 2, :].bitcast(F32), ALU.subtract).then_inc(gf_lo_ready, 1)

            def states(i, j, half, g=None):
                for c in ((1, 2) if half == 0 else range(3, NV)):
                    at = STATE_STEPS * i + 2 * (c - 1)
                    if c == 1:
                        dve.wait_ge(v_copied, i + 1)
                    else:
                        dve.wait_ge(state_chain, at)
                    dve.scalar_tensor_tensor(out=state[:, c, :], in0=state[:, c - 1, :],
                                             scalar=tab[:, j % UNROLL, LAM_RE:LAM_RE + 1], in1=state[:, c, :],
                                             op0=ALU.mult, op1=ALU.add).then_inc(state_chain, 1)
                    if g is not None and j == 1:
                        for n in ANGLES_AT[c]:
                            angle_step(g, n)
                    if g is not None and j == 3:
                        for n in K_AT[c]:
                            k_step(g, n)
                    dve.wait_ge(state_chain, at + 1)
                    dve.wait_ge(cross_ready, (NV - 1) * i + c)
                    dve.tensor_tensor(state[:, c, :], state[:, c, :], cross[:], ALU.add).then_inc(state_chain, 1)
                a, b = (0, HALF - 1) if half == 0 else (HALF - 1, NV)
                dve.wait_ge(s_hi_ready, 2 * i + half + 1)
                dve.tensor_tensor(s_lo[:, a:b, :], state[:, a:b, :], s_hi[:, a:b, :].bitcast(F32),
                                  ALU.subtract).then_inc(s_lo_ready, 1)

            def mask_y(i, half):
                dve.wait_ge(conv_done, 2 * i + half + 1)
                c = slice(half * HALF, (half + 1) * HALF)
                dve.tensor_tensor(ym[:, c, :], ps_y[half][:].rearrange(chunked, c=HALF),
                                  mask_cols[:, c, :], ALU.mult).then_inc(y_masked, 1)

            def split_y(i, half):
                dve.wait_ge(y_hi_ready, 2 * i + half + 1)
                c = slice(half * HALF, (half + 1) * HALF)
                dve.tensor_tensor(y_lo[:, c, :], ym[:, c, :], y_hi[:, c, :].bitcast(F32),
                                  ALU.subtract).then_inc(y_lo_ready, 1)

            def route(i):
                done = [0]

                def then(ins):
                    done[0] += 1
                    ins.then_inc(route_chain, 1)
                    dve.wait_ge(route_chain, ROUTE_STEPS * i + done[0])

                dve.wait_ge(h_done, i + 1)
                then(dve.tensor_copy(logit[:], ps_base[2][:, R0:R0 + E]))
                then(dve.tensor_reduce(top[:], logit[:], AX_X, ALU.max))
                dve.tensor_scalar(below[:], logit[:], top[:, 0:1], None, ALU.subtract).then_inc(below_ready, 1)
                then(dve.tensor_tensor(before[:], logit[:].unsqueeze(1).broadcast_to([P, E, E]),
                                       logit[:].unsqueeze(2).broadcast_to([P, E, E]), ALU.is_ge))
                then(dve.tensor_tensor(before[:], before[:], lower[:], ALU.mult))
                then(dve.tensor_tensor(balance[:], before[:], before[:].rearrange("p e f -> p f e"), ALU.subtract))
                then(dve.tensor_reduce(rank[:], balance[:], AX_X, ALU.add))
                then(dve.tensor_tensor(gate[:], rank[:], rank_limit[:], ALU.is_lt))
                dve.wait_ge(weight_ready, i + 1)
                then(dve.tensor_tensor(gate[:], gate[:], weight[:], ALU.mult))
                then(dve.tensor_reduce(total[:], gate[:], AX_X, ALU.add))
                then(dve.reciprocal(total[:], total[:]))
                assert done[0] == ROUTE_STEPS
                dve.scalar_tensor_tensor(out=hw[:], in0=ps_base[2][:, A0:A0 + ER].rearrange("p (e r) -> p e r", e=E),
                                         scalar=total[:, 0:1], in1=gate[:].unsqueeze(2).broadcast_to([P, E, R]),
                                         op0=ALU.mult, op1=ALU.mult).then_inc(hw_ready, 1)

            def split_hw(i):
                dve.wait_ge(hwt_hi_ready, i + 1)
                dve.tensor_tensor(hwt_lo[:], ps_h[:, 0:P], hwt_hi[:].bitcast(F32),
                                  ALU.subtract).then_inc(hwt_lo_ready, 1)

            def sum_out(i, j):
                dve.wait_ge(x_biased, i + 1)
                for s_ in range(3):
                    dve.wait_ge(lora_done, 3 * i + s_ + 1)
                    a, b = LSEG[s_], LSEG[s_ + 1]
                    dve.tensor_tensor(x_slot[:, j, a:b], ps_base[s_][:, 0:b - a], x_slot[:, j, a:b],
                                      ALU.add).then_inc(out_ready[s_], 1)

            dve.wait_ge(lens_in, 32)
            dve.tensor_copy(len_colf[:], len_col[:]).then_inc(lens_float, 1)
            dve.tensor_copy(len_rowf[:], len_row[:]).then_inc(lens_float, 1)
            dve.wait_ge(params_in, 64)
            s = [v[:, 0:N] for v in small]
            ex = small[6]
            exponential(lin[:], N + 1, ex[:], None, small[0][:], small[1][:], small[7][:])
            mag, dt = ex[:, 0:N], ex[:, N:N + 1]
            a_nat, w_nat = nat[:, 0, 0, :], nat[:, 1, 0, :]
            ts(a_nat, mag, dt, -1.0, ALU.mult, ALU.mult)
            ts(w_nat, aim[:], dt, None, ALU.mult, ALU.bypass)
            ts(s[2], w_nat, 1.0, None, ALU.mult, ALU.bypass)
            reduce_angle(link, s[2], s[3])
            ts(s[2], s[2], -PI_BELOW, PI_BELOW, ALU.max, ALU.min)
            magnitude(s[3], s[2]).then_inc(half_angle, 1)
            exponential(a_nat, N, None, s[8], s[0], s[1], s[7])
            dve.wait_ge(half_sin, 2)
            sn, cs, em1 = s[4], s[5], s[8]
            tt(s[0], sn, sn, ALU.mult)
            ts(s[0], s[0], -2.0, None, ALU.mult, ALU.bypass)
            stt(s[1], s[0], 1.0, em1, ALU.add, ALU.mult)
            tt(s[1], s[1], s[0], ALU.add)
            tt(s[2], sn, cs, ALU.mult)
            stt(s[2], em1, 1.0, s[2], ALU.add, ALU.mult)
            ts(s[2], s[2], 2.0, None, ALU.mult, ALU.bypass)
            c_re, c_im = cc[:, :, 0], cc[:, :, 1]
            tt(s[3], c_re, s[1], ALU.mult)
            tt(s[4], c_im, s[2], ALU.mult)
            tt(s[3], s[3], s[4], ALU.subtract)
            tt(s[4], c_re, s[2], ALU.mult)
            tt(s[5], c_im, s[1], ALU.mult)
            tt(s[4], s[4], s[5], ALU.add)
            tt(s[0], mag, mag, ALU.mult)
            tt(s[1], aim[:], aim[:], ALU.mult)
            tt(s[0], s[0], s[1], ALU.add)
            link(dve.reciprocal(s[0], s[0]))
            tt(s[1], s[4], aim[:], ALU.mult)
            tt(s[2], s[3], mag, ALU.mult)
            tt(s[1], s[1], s[2], ALU.subtract)
            tt(s[2], s[3], aim[:], ALU.mult)
            tt(s[5], s[4], mag, ALU.mult)
            stt(s[2], s[2], -1.0, s[5], ALU.mult, ALU.subtract)
            stt(nat[:, 2, 0, :], s[1], 2.0, s[0], ALU.mult, ALU.mult)
            stt(nat[:, 3, 0, :], s[2], 2.0, s[0], ALU.mult, ALU.mult)
            stt(nat[:, 4, 0, :], s[1], -2.0, s[0], ALU.mult, ALU.mult)
            dve.tensor_copy(nat[:, :, 1, :], nat[:, :, 0, :]).then_inc(nat_ready, 1)
            for u in range(UNITS_1):
                weight_low(u)
            dve.wait_ge(nat_turned, 1)
            turned = ps_h[:, 0:5 * H].rearrange("p (k h two) -> p k h two", k=5, two=2)
            dve.tensor_copy(coef[0:N, :, :], turned[0:N, :, :, 0]).then_inc(coef_ready, 1)
            dve.tensor_copy(coef[N:P, :, :], turned[N:P, :, :, 1]).then_inc(coef_ready, 1)
            dve.wait_ge(coef_ready, 2)
            dve.wait_ge(const_ready, 6)
            for n in range(ANGLE_STEPS):
                angle_step(0, n, first=True)
            for u in range(UNITS_1, UNITS_2):
                weight_low(u)
            dve.wait_ge(d_in, 16)
            for n in range(K_STEPS):
                k_step(0, n)
            split_u(0, 0)
            split_gf(0, 0)
            states(0, 0, 0)
            states(0, 0, 1)
            for u in range(UNITS_2, NUNITS):
                weight_low(u)
            split_u(1, 1)
            split_gf(1, 1)
            dve.wait_ge(masks_ready, NC)
            mask_y(0, 0)
            split_y(0, 0)
            mask_y(0, 1)
            split_y(0, 1)

            split_u(2, 2)
            split_gf(2, 2)

            def head(i, j, t=None):
                g = None if t is None else t + 1
                if i_left(i, 1):
                    states(i + 1, j + 1, 0, g)
                    states(i + 1, j + 1, 1, g)
                if j == 0 and t is not None:
                    angle_step(t + 1, 8)
                route(i)
                if i_left(i, 1):
                    mask_y(i + 1, 0)
                split_hw(i)
                if i_left(i, 1):
                    mask_y(i + 1, 1)
                    split_y(i + 1, 0)
                sum_out(i, j)
                if i_left(i, 1):
                    split_y(i + 1, 1)
                if i_left(i, 3):
                    split_u(i + 3, j + 3)
                    split_gf(i + 3, j + 3)

            with dve.Fori(0, H // UNROLL - 1) as t:
                for j in range(UNROLL):
                    head(UNROLL * t + j, j, t)
            for i in range(H - UNROLL, H):
                head(i, i % UNROLL)

        @block.tensor
        def _(pe):
            def turn_x(i):
                pe.wait_ge(x_masked, i + 1)
                for half in range(2):
                    for k in range(HALF):
                        c = half * HALF + k
                        mm = pe.transpose(ps_u[half][:, k * P:(k + 1) * P], xm[:, c * P:(c + 1) * P], ident[:])
                    mm.then_inc(u_turned, 1)

            def turn_g(i, j, loads):
                pe.wait_ge(tab_loaded[j % UNROLL], loads)
                pe.transpose(ps_h[:, 0:P], tab[:, j % UNROLL, 0:P], ident[:]).then_inc(g_turned, 1)

            def input_product(i, j):
                pe.wait_ge(u_lo_ready, 2 * i + 2)
                pe.wait_ge(gf_lo_ready, 2 * i + 2)
                for half in range(2):
                    a, b = half * HALF, min((half + 1) * HALF, NV)
                    for n, (g, u) in enumerate(((g_hi, u_hi), (g_hi, u_lo), (g_lo, u_hi))):
                        mm = pe.matmul(ps_u[half][:, 0:(b - a) * P], g[:], u[:, j % 2, a:b, :],
                                       start=(n == 0), stop=(n == 2))
                mm.then_inc(v_done, 1)

            def conv(i, j, half):
                c = slice(half * HALF, (half + 1) * HALF)
                for n, (part, u) in enumerate(((0, u_hi), (0, u_lo), (1, u_hi))):
                    pe.matmul(ps_y[half][:], toep[:, j % UNROLL, part, :], u[:, j % 2, c, :],
                              start=(n == 0), stop=False)
                a, b = (0, HALF - 1) if half == 0 else (HALF - 1, NV)
                pe.wait_ge(s_lo_ready, 2 * i + half + 1)
                for n, (f, s) in enumerate(((f_hi, s_hi), (f_hi, s_lo), (f_lo, s_hi))):
                    mm = pe.matmul(ps_y[half][:, BANK - (b - a) * P:BANK], f[:, j % 2, :], s[:, a:b, :],
                                   start=False, stop=(n == 2))
                mm.then_inc(conv_done, 1)

            def linear(chunks, pieces):
                for s in pieces:
                    for c in chunks:
                        for n, (y, w) in enumerate(((y_hi, w_hi), (y_hi, w_lo), (y_lo, w_hi))):
                            mm = pe.matmul(ps_base[s][:, 0:SEG[s + 1] - SEG[s]], y[:, c, :],
                                           w[:, c, SEG[s]:SEG[s + 1]], start=(c == 0 and n == 0),
                                           stop=(c == NC - 1 and n == 2))
                return mm

            def linear_start(i, first=False):
                pe.wait_ge(y_lo_ready, 2 * i + 1)
                for s in range(3):
                    if not first:
                        pe.wait_ge(out_ready[s], i)
                    linear(range(2), [s])

            def turn_hw(i):
                pe.wait_ge(hw_ready, i + 1)
                pe.transpose(ps_h[:, 0:P], hw[:].rearrange("p e r -> p (e r)"), ident[:]).then_inc(hw_turned, 1)

            def lora(i):
                pe.wait_ge(hwt_lo_ready, i + 1)
                for s in range(3):
                    a, b = LSEG[s], LSEG[s + 1]
                    for n, (h, w) in enumerate(((hwt_hi, b2_hi), (hwt_hi, b2_lo), (hwt_lo, b2_hi))):
                        mm = pe.matmul(ps_base[s][:, 0:b - a], h[:], w[:, a:b], start=False, stop=(n == 2),
                                       skip_group_check=True)
                    mm.then_inc(lora_done, 1)

            def sum_k(g):
                pe.wait_ge(comb_ready, g + 1)
                pe.matmul(k_bank, parity[:], comb[:, 0, :, FCOL:FCOL + P], start=True,
                          stop=True).then_inc(k_summed, 1)

            pe.wait_ge(const_ready, 1)
            for u in range(UNITS_1):
                weight_unit(pe, u)
            pe.wait_ge(nat_ready, 1)
            for k in range(5):
                mm = pe.transpose(ps_h[:, k * H:(k + 1) * H], nat[:, k, :, :].rearrange("h two n -> h (two n)"),
                                  ident[0:H, 0:H])
            mm.then_inc(nat_turned, 1)
            for u in range(UNITS_1, UNITS_2):
                weight_unit(pe, u)
            pe.wait_ge(const_ready, 6)
            sum_k(0)
            turn_x(0)
            pe.wait_ge(k_ready, 1)
            turn_g(0, 0, 16)
            input_product(0, 0)
            for u in range(UNITS_2, NUNITS):
                weight_unit(pe, u)
            pe.wait_ge(wt_lo_ready, NUNITS)
            pe.wait_ge(v_copied, 1)
            turn_x(1)
            turn_g(1, 1, 16)
            pe.wait_ge(toep_loaded[0], 16)
            conv(0, 0, 0)
            conv(0, 0, 1)
            input_product(1, 1)
            pe.wait_ge(v_copied, 2)
            turn_x(2)
            turn_g(2, 2, 16)
            linear_start(0, first=True)

            def head(i, j, t=None):
                def loads(ahead):
                    return 16 * (H // UNROLL) if t is None else 16 * t + 16 + 16 * ((j + ahead) // UNROLL)

                linear(range(2, HALF), [0])
                if j == 2 and t is not None:
                    pe.wait_ge(gf_lo_ready, 2 * i + 6)
                    sum_k(t + 1)
                linear(range(2, HALF), [1, 2])
                pe.wait_ge(y_lo_ready, 2 * i + 2)
                linear(range(HALF, NC), [2]).then_inc(h_done, 1)
                if i_left(i, 2):
                    input_product(i + 2, j + 2)
                linear(range(HALF, NC), [0, 1])
                if i_left(i, 1):
                    pe.wait_ge(toep_loaded[(j + 1) % UNROLL], loads(1))
                    conv(i + 1, j + 1, 0)
                if j == 2 and t is not None:
                    pe.wait_ge(k_ready, 2 * t + 3)
                turn_hw(i)
                if i_left(i, 1):
                    conv(i + 1, j + 1, 1)
                lora(i)
                if i_left(i, 3):
                    pe.wait_ge(v_copied, i + 3)
                    turn_x(i + 3)
                    turn_g(i + 3, j + 3, loads(3))
                if i_left(i, 1):
                    linear_start(i + 1)

            with pe.Fori(0, H // UNROLL - 1) as t:
                for j in range(UNROLL):
                    head(UNROLL * t + j, j, t)
            for i in range(H - UNROLL, H):
                head(i, i % UNROLL)


_INS = ['x', 'itok_B_8_3872', 'L0_cond_log_dt', 'L0_cond_C', 'L0_cond_log_A_real', 'L0_cond_A_imag', 'L0_cond_D',
        'L0_ffn_W_base', 'L0_ffn_b_base', 'L0_ffn_W_router', 'L0_ffn_A', 'L0_ffn_B']


def kernel(**inputs):
    import concourse.bacc as _bacc
    from concourse.bass_utils import run_bass_kernel_spmd as _run

    nc = _bacc.Bacc("TRN2", target_bir_lowering=False, num_devices=1)
    arrays, args = {}, []
    for name in _INS:
        a = np.ascontiguousarray(inputs[name])
        arrays[f"in_{name}_dram"] = a
        args.append(nc.dram_tensor(f"in_{name}_dram", a.shape, mybir.dt.from_np(a.dtype), kind="ExternalInput").ap())
    args.append(nc.dram_tensor("out_0_dram", inputs['x'].shape, F32, kind="ExternalOutput").ap())
    s4d_lora_ffn(nc, *args)
    r = _run(nc, [arrays], core_ids=[0])
    return r.results[0]["out_0_dram"]
```

```python
from contextlib import ExitStack
import math

import numpy as np
import concourse.bass as bass
from concourse import mybir

F32 = mybir.dt.float32
F32R = mybir.dt.float32r
I32 = mybir.dt.int32
AX_X = mybir.AxisListType.X
ALU = mybir.AluOpType
ACT = mybir.ActivationFunctionType

P = 128
BANK = 512
MAGIC = 1.5 * 2.0 ** 23
LOG2E = 1.0 / math.log(2.0)
LN2_HI = 0.693359375
LN2_LO = math.log(2.0) - LN2_HI
TWO_PI_1 = 6.28125
TWO_PI_2 = math.floor((2 * math.pi - TWO_PI_1) * 2.0 ** 20) / 2.0 ** 20
TWO_PI_3 = 2 * math.pi - TWO_PI_1 - TWO_PI_2
PI_BELOW = 3.1415925


def s4d_lora_ffn(nc, x, lengths, log_dt, C, log_A_real, A_imag, D, W_base, b_base, W_router, A_lora, B_lora, out):
    B, H, L = x.shape
    N = A_imag.shape[1]
    E, R, _ = A_lora.shape
    O = W_base.shape[0]
    ER = E * R
    NC = L // P
    HALF = NC // 2
    HC = HALF * P
    assert B == P and ER == P and 2 * N == P and HC == BANK and O == L and H % 4 == 0
    SCALING = 32.0 / R
    COLS = O + ER + E
    SEG = [0, 388, 776, COLS]
    LSEG = [0, 388, 776, O]
    A0, R0 = O - SEG[2], O + ER - SEG[2]
    HP = H // 2
    NV = NC - 1
    UNROLL = 4
    GP = UNROLL // 2
    NPOS = P + 1
    LAM_RE, FCOL, LAM_IM = P, NPOS, 2 * NPOS
    TROW = 2 * NPOS + 2
    KROW = 2 * P
    ROUTE_STEPS, GEN_STEPS, TAB_STEPS, KSUM_STEPS = 9, 6, 6, 2
    STATE_STEPS = 2 * (NV - 1)
    ANGLE_STEPS, K_STEPS = 9, 4
    ANGLES_AT = ((), (0, 1), (2,), (3,), (4,), (5,), (6, 7))
    K_AT = ((), (), (), (0,), (1,), (2,), (3,))

    tab_dram = nc.dram_tensor("tab_dram", [H, P, TROW], F32, kind="Internal")
    k_dram = nc.dram_tensor("k_dram", [H, 2, KROW], F32, kind="Internal")

    with ExitStack() as ctx:
        def sb(name, shape, dt=F32):
            return ctx.enter_context(nc.sbuf_tensor(name, shape, dt))

        def sem(name):
            return ctx.enter_context(nc.semaphore(name))

        w_hi = sb("w_hi", [P, NC, COLS], F32R)
        w_lo = sb("w_lo", [P, NC, COLS], F32R)
        b2_hi = sb("b2_hi", [P, O], F32R)
        b2_lo = sb("b2_lo", [P, O], F32R)
        bias_rows = sb("bias_rows", [P, O])
        mask_rows = sb("mask_rows", [P, L])
        mask_cols = sb("mask_cols", [P, NC, P])
        ident = sb("ident", [P, P])
        lower = sb("lower", [P, E, E])
        rank_limit = sb("rank_limit", [P, E])
        half_pi = sb("half_pi", [P, 1])
        preloaded = sb("preloaded", [P, 2])
        pos = sb("pos", [P, NPOS])
        parity = sb("parity", [P, 2])
        signs = sb("signs", [P, 2, GP])
        coef = sb("coef", [P, 5, HP])
        d_rows = sb("d_rows", [2, HP])
        x_slot = sb("x_slot", [P, UNROLL, L])
        xm = sb("xm", [P, L])
        u_hi = sb("u_hi", [P, 2, NC, P], F32R)
        u_lo = sb("u_lo", [P, 2, NC, P], F32R)
        ym = sb("ym", [P, NC, P])
        y_hi = sb("y_hi", [P, NC, P], F32R)
        y_lo = sb("y_lo", [P, NC, P], F32R)
        tab = sb("tab", [P, UNROLL, TROW])
        toep = sb("toep", [P, UNROLL, 2, P], F32R)
        g_hi = sb("g_hi", [P, P], F32R)
        g_lo = sb("g_lo", [P, P], F32R)
        f_hi = sb("f_hi", [P, 2, P], F32R)
        f_lo = sb("f_lo", [P, 2, P], F32R)
        state = sb("state", [P, NV, P])
        cross = sb("cross", [P, P])
        s_hi = sb("s_hi", [P, NV, P], F32R)
        s_lo = sb("s_lo", [P, NV, P], F32R)
        logit = sb("logit", [P, E])
        top = sb("top", [P, 1])
        below = sb("below", [P, E])
        weight = sb("weight", [P, E])
        before = sb("before", [P, E, E])
        balance = sb("balance", [P, E, E])
        rank = sb("rank", [P, E])
        gate = sb("gate", [P, E])
        total = sb("total", [P, 1])
        hw = sb("hw", [P, E, R])
        hwt_hi = sb("hwt_hi", [P, P], F32R)
        hwt_lo = sb("hwt_lo", [P, P], F32R)
        cur = sb("cur", [P, 5, GP])
        theta = sb("theta", [P, GP, NPOS])
        turns = sb("turns", [P, GP, NPOS])
        decay = sb("decay", [P, GP, NPOS])
        sines = sb("sines", [P, GP, NPOS])
        cosines = sb("cosines", [P, GP, NPOS])
        term_a = sb("term_a", [P, GP, NPOS])
        term_b = sb("term_b", [P, GP, NPOS])
        comb = sb("comb", [P, 2, GP, TROW])
        k_full = sb("k_full", [2, GP, P])
        k_split = sb("k_split", [2, 2, GP, P], F32R)
        stage = sb("stage", [P, 4, L])
        nat = sb("nat", [N, 5, 2, N])
        lin = sb("lin", [H, N + 1])
        aim = sb("aim", [H, N])
        cc = sb("cc", [H, N, 2])
        small = [sb(f"small{i}", [H, N + 1]) for i in range(10)]
        ki = sb("ki", [H, N + 1], I32)
        len_col = sb("len_col", [P, 1], I32)
        len_colf = sb("len_colf", [P, 1])
        len_row = sb("len_row", [P, P], I32)
        len_rowf = sb("len_rowf", [P, P])
        chunk_pos = sb("chunk_pos", [P, NC])
        zeros = state[0:H, 0:2, :]
        router_stage = ym[0:E, :, :].rearrange("e c n -> e (c n)")

        def bank(name):
            return ctx.enter_context(nc.psum_tensor(name, [P, BANK], F32))

        ps_base = [bank(f"ps_base{s}") for s in range(3)]
        ps_y = [bank(f"ps_y{s}") for s in range(2)]
        ps_u = [bank(f"ps_u{s}") for s in range(2)]
        ps_h = bank("ps_h")
        k_bank = ps_h[0:2, P:P + GP * P]

        lin_in = sem("lin_in")
        aim_c_in = sem("aim_c_in")
        lens_in = sem("lens_in")
        bias_in = sem("bias_in")
        d_in = sem("d_in")
        stage_in = [sem(f"stage_in{i}") for i in range(4)]
        router_in = sem("router_in")
        const_ready = sem("const_ready")
        zeros_ready = sem("zeros_ready")
        masks_ready = sem("masks_ready")
        pool_chain = sem("pool_chain")
        dve_chain = sem("dve_chain")
        half_angle = sem("half_angle")
        half_sin = sem("half_sin")
        nat_ready = sem("nat_ready")
        nat_turned = sem("nat_turned")
        coef_ready = sem("coef_ready")
        pad_stored = sem("pad_stored")
        wt_turned = sem("wt_turned")
        wt_hi_ready = sem("wt_hi_ready")
        pool_low = sem("pool_low")
        dve_low = sem("dve_low")
        cur_ready = sem("cur_ready")
        gen_chain = sem("gen_chain")
        angle_ready = sem("angle_ready")
        decay_arg = sem("decay_arg")
        sincos_ready = sem("sincos_ready")
        tab_chain = sem("tab_chain")
        comb_ready = sem("comb_ready")
        tab_stored = sem("tab_stored")
        k_summed = sem("k_summed")
        ksum_chain = sem("ksum_chain")
        k_ready = sem("k_ready")
        k_stored = sem("k_stored")
        x_loaded = [sem(f"x_loaded{i}") for i in range(UNROLL)]
        tab_loaded = [sem(f"tab_loaded{i}") for i in range(UNROLL)]
        toep_loaded = [sem(f"toep_loaded{i}") for i in range(UNROLL)]
        stored = [sem(f"stored{i}") for i in range(UNROLL)]
        x_masked = sem("x_masked")
        x_biased = sem("x_biased")
        u_turned = sem("u_turned")
        u_hi_ready = sem("u_hi_ready")
        u_lo_ready = sem("u_lo_ready")
        g_turned = sem("g_turned")
        gf_hi_ready = sem("gf_hi_ready")
        g_lo_ready = sem("g_lo_ready")
        f_lo_ready = sem("f_lo_ready")
        v_done = sem("v_done")
        v_copied = sem("v_copied")
        cross_ready = sem("cross_ready")
        state_chain = sem("state_chain")
        s_hi_ready = sem("s_hi_ready")
        s_lo_ready = sem("s_lo_ready")
        conv_done = sem("conv_done")
        y_masked = sem("y_masked")
        y_hi_ready = sem("y_hi_ready")
        y_lo_ready = [sem(f"y_lo_ready{half}") for half in range(2)]
        h_done = sem("h_done")
        below_ready = sem("below_ready")
        weight_ready = sem("weight_ready")
        route_chain = sem("route_chain")
        hw_ready = sem("hw_ready")
        hw_turned = sem("hw_turned")
        hwt_hi_ready = sem("hwt_hi_ready")
        hwt_lo_ready = sem("hwt_lo_ready")
        lora_done = sem("lora_done")
        out_ready = [sem(f"out_ready{s}") for s in range(3)]

        NB = O // P
        blocks = [(W_base[P * i:P * (i + 1), :], P * i) for i in range(NB)]
        blocks.append((A_lora.rearrange("e r d -> (e r) d"), O))
        units = [(i, col, c0) for i, (_, col) in enumerate(blocks) for c0 in (0, HALF)]
        B_UNIT = len(units)
        NUNITS = B_UNIT + 3
        b_slot = len(blocks) % 4
        unit_bank = [ps_base[0], ps_base[1], ps_base[2], ps_y[1]]
        POOL_UNITS = 8
        U_SIN, U_NAT, U_X0, U_S0 = 1, 8, 14, NUNITS - (NV - 1)

        def unit_copy(u):
            return x_slot[:, 2 + (u % 4) // 2, (u % 2) * HC:(u % 2 + 1) * HC]

        def weight_unit(pe, u):
            if u >= 4:
                v = u - 4
                if v < POOL_UNITS:
                    pe.wait_ge(wt_hi_ready, v + 1)
                else:
                    pe.wait_ge(dve_low, v - POOL_UNITS + 1)
            dst = unit_bank[u % 4]
            if u < B_UNIT:
                blk, _, c0 = units[u]
                pe.wait_ge(stage_in[blk % 4], 16 * (blk // 4 + 1))
                for k in range(HALF):
                    mm = pe.transpose(dst[:, k * P:(k + 1) * P], stage[:, blk % 4, (c0 + k) * P:(c0 + k + 1) * P],
                                      ident[:])
            elif u < B_UNIT + 2:
                pe.wait_ge(stage_in[b_slot], 16 * (len(blocks) // 4) + 16 * E)
                for k in range(HALF):
                    c = (u - B_UNIT) * HALF + k
                    mm = pe.transpose(dst[:, k * P:(k + 1) * P], stage[:, b_slot, c * P:(c + 1) * P], ident[:])
            else:
                pe.wait_ge(router_in, 16)
                for c in range(NC):
                    mm = pe.transpose(dst[:, c * E:(c + 1) * E], router_stage[:, c * P:(c + 1) * P], ident[0:E, 0:E])
            mm.then_inc(wt_turned, 1)

        def unit_views(u):
            src = unit_bank[u % 4]
            if u < B_UNIT:
                _, col, c0 = units[u]
                return (src[:].rearrange("p (c n) -> p c n", c=HALF), w_hi[:, c0:c0 + HALF, col:col + P],
                        w_lo[:, c0:c0 + HALF, col:col + P], 1.0)
            if u < B_UNIT + 2:
                at = (u - B_UNIT) * HC
                return src[:], b2_hi[:, at:at + HC], b2_lo[:, at:at + HC], SCALING
            return (src[:, 0:NC * E].rearrange("p (c n) -> p c n", c=NC), w_hi[:, :, O + ER:COLS],
                    w_lo[:, :, O + ER:COLS], 1.0)

        def tab_source(h):
            return tab_dram[h, :, 0:TROW - 1]

        def toeplitz_source(h):
            return bass.AP(k_dram, h * (2 * KROW) + 1, [[1, P], [KROW, 2], [1, P]])

        def i_left(i, ahead):
            return not isinstance(i, int) or i + ahead < H

        def over_pairs(q):
            return cur[:, q, :].unsqueeze(2).broadcast_to([P, GP, NPOS])

        def tables(engine, g, first=False):
            done = [0]

            def then(ins):
                done[0] += 1
                ins.then_inc(tab_chain, 1)
                engine.wait_ge(tab_chain, TAB_STEPS * g + done[0])

            if not first:
                engine.wait_ge(tab_stored, 64 * g)
                engine.wait_ge(k_summed, g)
            engine.wait_ge(sincos_ready, 3 * g + 3)
            e_re, e_im = comb[:, 0, :, 0:NPOS], comb[:, 1, :, 0:NPOS]
            f_re, f_im = comb[:, 0, :, FCOL:FCOL + NPOS], comb[:, 1, :, FCOL:FCOL + NPOS]
            engine.tensor_tensor(e_im, decay[:], sines[:], ALU.mult)
            then(engine.tensor_tensor(e_re, decay[:], cosines[:], ALU.mult))
            engine.tensor_tensor(term_a[:], e_re, over_pairs(2), ALU.mult)
            then(engine.tensor_tensor(term_b[:], e_im, over_pairs(3), ALU.mult))
            then(engine.tensor_tensor(f_re, term_a[:], term_b[:], ALU.subtract))
            engine.tensor_tensor(term_a[:], e_im, over_pairs(4), ALU.mult)
            then(engine.tensor_tensor(term_b[:], e_re, over_pairs(3), ALU.mult))
            then(engine.tensor_tensor(f_im, term_a[:], term_b[:], ALU.subtract))
            then(engine.tensor_tensor(comb[:, :, :, LAM_IM], comb[:, 1, :, P].unsqueeze(1).broadcast_to([P, 2, GP]),
                                      signs[:], ALU.mult))
            assert done[0] == TAB_STEPS
            engine.tensor_tensor(comb[:, 1, :, LAM_RE], comb[:, 0, :, LAM_RE], signs[:, 0, :],
                                 ALU.mult).then_inc(comb_ready, 1)

        def low_states(engine, i, half):
            a, b = (0, HALF - 1) if half == 0 else (HALF - 1, NV)
            engine.wait_ge(s_hi_ready, 2 * i + half + 1)
            engine.tensor_tensor(s_lo[:, a:b, :], state[:, a:b, :], s_hi[:, a:b, :].bitcast(F32),
                                 ALU.subtract).then_inc(s_lo_ready, 1)

        def low_y(engine, i, half):
            engine.wait_ge(y_hi_ready, 2 * i + half + 1)
            c = slice(half * HALF, (half + 1) * HALF)
            engine.tensor_tensor(y_lo[:, c, :], ym[:, c, :], y_hi[:, c, :].bitcast(F32),
                                 ALU.subtract).then_inc(y_lo_ready[half], 1)

        def low_f(engine, i, j):
            engine.wait_ge(gf_hi_ready, 2 * i + 2)
            engine.tensor_tensor(f_lo[:, j % 2, :], tab[:, j % UNROLL, FCOL + 1:FCOL + NPOS],
                                 f_hi[:, j % 2, :].bitcast(F32), ALU.subtract).then_inc(f_lo_ready, 1)

        xm_reversed = bass.AP(xm, P - 1, [[L, P], [P, NC], [-1, P]])
        chunked = "p (c n) -> p c n"
        block = ctx.enter_context(nc.Block())

        @block.sync
        def _(sp):
            def load_tab(h, j):
                sp.dma_start(tab[:, j, 0:TROW - 1], tab_source(h)).then_inc(tab_loaded[j], 16)

            def load_toep(h, j):
                sp.dma_start(toep[:, j, :, :].bitcast(F32), toeplitz_source(h)).then_inc(toep_loaded[j], 16)

            def store_tables(g):
                sp.wait_ge(comb_ready, g + 1)
                for par in range(2):
                    for half in range(2):
                        dst = bass.AP(tab_dram, (g * UNROLL + par) * (P * TROW) + half * N * TROW,
                                      [[TROW, N], [2 * P * TROW, GP], [1, TROW - 1]])
                        sp.dma_start(dst, comb[N * par:N * (par + 1), half, :, 0:TROW - 1]).then_inc(tab_stored, 16)

            def store_k(g):
                sp.wait_ge(k_ready, 2 * g + 2)
                for part in range(2):
                    dst = bass.AP(k_dram, (g * UNROLL) * (2 * KROW) + part * KROW + P,
                                  [[2 * KROW, 2], [4 * KROW, GP], [1, P]])
                    sp.dma_start(dst, k_split[:, part, :, :].bitcast(F32)).then_inc(k_stored, 16)

            sp.dma_start(lin[:, 0:N], log_A_real).then_inc(lin_in, 16)
            sp.dma_start(lin[:, N:N + 1], log_dt.rearrange("(h o) -> h o", o=1)).then_inc(lin_in, 16)
            sp.dma_start(aim[:], A_imag).then_inc(aim_c_in, 16)
            sp.dma_start(cc[:], C).then_inc(aim_c_in, 16)
            sp.dma_start(len_col[:], lengths.rearrange("(b o) -> b o", o=1)).then_inc(lens_in, 16)
            sp.dma_start(len_row[:], bass.AP(lengths.tensor, 0, [[0, P], [1, B]])).then_inc(lens_in, 16)
            for i in range(4):
                sp.dma_start(stage[:, i, :], blocks[i][0]).then_inc(stage_in[i], 16)
            sp.dma_start(x_slot[:, 0, :], x[:, 0, :]).then_inc(x_loaded[0], 16)
            with nc.allow_non_contiguous_dma(reason="64 values, once"):
                sp.dma_start(d_rows[:], D.rearrange("(g two) -> two g", two=2)).then_inc(d_in, 16)
            sp.dma_start(router_stage, W_router).then_inc(router_in, 16)
            sp.wait_ge(zeros_ready, 1)
            sp.dma_start(bass.AP(k_dram, 0, [[2 * KROW, H], [KROW, 2], [1, P]]), zeros).then_inc(pad_stored, 16)

            def next_block(i):
                sp.wait_ge(wt_turned, 2 * (i - 4) + 2)
                if i < len(blocks):
                    sp.dma_start(stage[:, i % 4, :], blocks[i][0]).then_inc(stage_in[i % 4], 16)
                else:
                    for e in range(E):
                        dst = stage[:, b_slot, :].rearrange("p (c e r) -> p c e r", c=NB, e=E)[:, :, e, :]
                        sp.dma_start(dst, B_lora[e].rearrange("(c p) r -> p c r", p=P)).then_inc(stage_in[b_slot], 16)

            next_block(4)
            sp.dma_start(bias_rows[:], bass.AP(b_base.tensor, 0, [[0, P], [1, O]])).then_inc(bias_in, 16)
            for i in range(5, 8):
                next_block(i)
            sp.dma_start(x_slot[:, 1, :], x[:, 1, :]).then_inc(x_loaded[1], 16)
            for i in range(8, len(blocks) + 1):
                next_block(i)
            sp.wait_ge(pool_low, POOL_UNITS)
            for h in range(2, UNROLL):
                sp.dma_start(x_slot[:, h, :], x[:, h, :]).then_inc(x_loaded[h], 16)
            store_tables(0)
            store_k(0)
            sp.wait_ge(tab_stored, 64)
            for h in range(1, UNROLL - 1):
                load_tab(h, h)
            sp.wait_ge(pad_stored, 16)
            sp.wait_ge(k_stored, 32)
            for h in range(2):
                load_toep(h, h)

            def head(i, j, g=None, last=False):
                if j == 1 and not last:
                    store_tables(g)
                    sp.wait_ge(tab_stored, 64 * g + 64)
                if not last or j + 3 < UNROLL:
                    load_tab(i + 3, (j + 3) % UNROLL)
                if j == 2 and not last:
                    store_k(g)
                    sp.wait_ge(k_stored, 32 * g + 32)
                if not last or j + 2 < UNROLL:
                    load_toep(i + 2, (j + 2) % UNROLL)
                last_head = last and j == UNROLL - 1
                for s in range(3):
                    sp.wait_ge(out_ready[s], i + 1)
                    if last_head:
                        a, b = LSEG[s], LSEG[s + 1]
                        sp.dma_start(out[:, i, a:b], x_slot[:, j, a:b]).then_inc(stored[j], 16)
                if not last_head:
                    sp.dma_start(out[:, i, :], x_slot[:, j, :]).then_inc(stored[j], 16)

            with sp.Fori(0, H // UNROLL - 1) as t:
                for j in range(UNROLL):
                    i = UNROLL * t + j
                    head(i, j, t + 1)
                    sp.wait_ge(stored[j], 16 * t + 16)
                    sp.dma_start(x_slot[:, j, :], x[:, i + UNROLL, :]).then_inc(x_loaded[j], 16)
            for j in range(UNROLL):
                head(H - UNROLL + j, j, last=True)
            for j in range(UNROLL):
                sp.wait_ge(stored[j], 16 * (H // UNROLL) + (32 if j == UNROLL - 1 else 0))

        @block.gpsimd
        def _(pool):
            count = [0]

            def link(ins):
                count[0] += 1
                ins.then_inc(pool_chain, 1)
                pool.wait_ge(pool_chain, count[0])

            def iota(dst, pattern, base=0, channel=0):
                return pool.iota(dst, pattern, base=base, channel_multiplier=channel,
                                 allow_small_or_imprecise_dtypes=True)

            link(pool.memset(ident[:], 0.0))
            pool.affine_select(out=ident[:], in_=ident[:], compare_op=ALU.not_equal, fill=1.0, base=0,
                               pattern=[[-1, P]], channel_multiplier=1).then_inc(const_ready, 1)
            pool.memset(half_pi[:], math.pi / 2).then_inc(const_ready, 1)
            iota(pos[:], [[1, NPOS]]).then_inc(const_ready, 1)
            link(pool.memset(parity[:], 0.0))
            pool.memset(signs[:, 0, :], 1.0)
            pool.memset(signs[:, 1, :], -1.0)
            iota(rank_limit[:], [[1, E]], base=3 - E).then_inc(const_ready, 1)
            link(pool.memset(lower[:], 1.0))
            pool.affine_select(out=lower[:], in_=lower[:], compare_op=ALU.is_gt, fill=0.0, base=0,
                               pattern=[[1, E], [-1, E]], channel_multiplier=0).then_inc(const_ready, 1)
            pool.wait_ge(const_ready, 5)
            link(pool.memset(parity[0:N, 0:1], 1.0))
            pool.memset(parity[N:P, 1:2], 1.0).then_inc(const_ready, 1)
            pool.wait_ge(const_ready, 6)
            pool.memset(zeros, 0.0).then_inc(zeros_ready, 1)
            iota(chunk_pos[:], [[P, NC]], channel=1)
            link(iota(mask_rows[:], [[1, L]]))
            pool.wait_ge(lens_in, 32)
            pool.tensor_copy(len_colf[:], len_col[:])
            link(pool.tensor_copy(len_rowf[:], len_row[:]))
            link(pool.tensor_scalar(mask_rows[:], mask_rows[:], len_colf[:, 0:1], None, ALU.is_lt))

            def mask_x(i, j, loads):
                pool.wait_ge(x_loaded[j], loads)
                pool.tensor_tensor(xm_reversed, x_slot[:, j, :].rearrange(chunked, c=NC),
                                   mask_rows[:].rearrange(chunked, c=NC), ALU.mult).then_inc(x_masked, 1)

            def add_bias(i, j):
                pool.wait_ge(x_masked, i + 1)
                pool.tensor_tensor(x_slot[:, j, :], x_slot[:, j, :], bias_rows[:], ALU.add).then_inc(x_biased, 1)

            def decay_argument(g):
                pool.wait_ge(cur_ready, g + 1)
                pool.tensor_tensor(decay[:], over_pairs(0), pos[:].unsqueeze(1).broadcast_to([P, GP, NPOS]),
                                   ALU.mult).then_inc(decay_arg, 1)

            for u in range(POOL_UNITS):
                pool.wait_ge(wt_hi_ready, u + 1)
                _, hi, lo, _ = unit_views(u)
                pool.tensor_tensor(lo, unit_copy(u).rearrange(chunked, c=HALF), hi.bitcast(F32),
                                   ALU.subtract).then_inc(pool_low, 1)
            pool.wait_ge(const_ready, 6)
            decay_argument(0)
            pool.wait_ge(bias_in, 16)
            mask_x(0, 0, 16)
            add_bias(0, 0)
            for c in range(NC):
                ins = pool.tensor_scalar(mask_cols[:, c, :], len_rowf[:], chunk_pos[:, c:c + 1], None, ALU.is_gt)
                ins.then_inc(masks_ready, 1)
            low_f(pool, 0, 0)
            for h in (1, 2):
                pool.wait_ge(u_turned, 2 * h)
                mask_x(h, h, 16)
                add_bias(h, h)
            low_states(pool, 0, 1)
            low_f(pool, 1, 1)
            low_y(pool, 0, 1)

            def head(i, j, t=None):
                if i_left(i, 2):
                    low_f(pool, i + 2, j + 2)
                if j == 0 and t is not None:
                    decay_argument(t + 1)
                if i_left(i, 1):
                    low_states(pool, i + 1, 0)
                    low_states(pool, i + 1, 1)
                if i_left(i, 3):
                    pool.wait_ge(u_turned, 2 * i + 6)
                    loads = 16 * (H // UNROLL) if t is None else 16 * t + 16 + 16 * ((j + 3) // UNROLL)
                    mask_x(i + 3, (j + 3) % UNROLL, loads)
                    add_bias(i + 3, (j + 3) % UNROLL)
                if i_left(i, 1):
                    low_y(pool, i + 1, 1)
                if j == 0 and t is not None:
                    tables(pool, t + 1)

            with pool.Fori(0, H // UNROLL - 1) as t:
                for j in range(UNROLL):
                    head(UNROLL * t + j, j, t)
            for i in range(H - UNROLL, H - 1):
                head(i, i % UNROLL)

        @block.scalar
        def _(act):
            def weight_high(u):
                act.wait_ge(wt_turned, u + 1)
                src, hi, _, factor = unit_views(u)
                if u < POOL_UNITS:
                    if u >= 4:
                        act.wait_ge(pool_low, u - 3)
                    act.activation(unit_copy(u).rearrange(chunked, c=HALF), src, ACT.Copy)
                act.activation(hi, src, ACT.Copy, scale=factor).then_inc(wt_hi_ready, 1)

            def preload(function):
                c = 0 if function == ACT.Sin else 1
                act.activation(preloaded[:, c:c + 1], half_pi[:], function)

            def group_decay(g):
                act.wait_ge(decay_arg, g + 1)
                act.activation(decay[:], decay[:], ACT.Exp).then_inc(sincos_ready, 1)

            def group_sincos(g):
                act.wait_ge(angle_ready, 2 * g + 1)
                act.activation(sines[:], theta[:], ACT.Sin).then_inc(sincos_ready, 1)
                act.wait_ge(angle_ready, 2 * g + 2)
                act.activation(cosines[:], turns[:], ACT.Sin, scale=-1.0, bias=half_pi[:]).then_inc(sincos_ready, 1)

            def split_u(i, j):
                for half in range(2):
                    act.wait_ge(u_turned, 2 * i + half + 1)
                    c = slice(half * HALF, (half + 1) * HALF)
                    act.activation(u_hi[:, j % 2, c, :], ps_u[half][:].rearrange(chunked, c=HALF),
                                   ACT.Copy).then_inc(u_hi_ready, 1)

            def split_gf(i, j):
                act.wait_ge(g_turned, i + 1)
                act.activation(g_hi[:], ps_h[:, 0:P], ACT.Copy).then_inc(gf_hi_ready, 1)
                act.activation(f_hi[:, j % 2, :], tab[:, j % UNROLL, FCOL + 1:FCOL + NPOS],
                               ACT.Copy).then_inc(gf_hi_ready, 1)

            def copy_v(i):
                act.wait_ge(v_done, i + 1)
                act.activation(state[:, 0:HALF, :], ps_u[0][:].rearrange(chunked, c=HALF), ACT.Copy)
                act.activation(state[:, HALF:NV, :], ps_u[1][:, 0:(NV - HALF) * P].rearrange(chunked, c=NV - HALF),
                               ACT.Copy).then_inc(v_copied, 1)

            def cross_terms(i, j, c):
                if c == 1:
                    act.wait_ge(v_copied, i + 1)
                else:
                    act.wait_ge(state_chain, STATE_STEPS * i + 2 * (c - 1))
                lam = tab[:, j % UNROLL, LAM_IM:LAM_IM + 1]
                act.activation(cross[0:N, :], state[N:P, c - 1, :], ACT.Copy, scale=lam[N:P])
                act.activation(cross[N:P, :], state[0:N, c - 1, :], ACT.Copy, scale=lam[0:N]).then_inc(cross_ready, 1)

            def split_state(i, half):
                a, b = (0, HALF - 1) if half == 0 else (HALF - 1, NV)
                act.wait_ge(state_chain, STATE_STEPS * i + 2 * (b - 1))
                act.activation(s_hi[:, a:b, :], state[:, a:b, :], ACT.Copy).then_inc(s_hi_ready, 1)

            def states(i, j, half):
                for c in ((1, 2) if half == 0 else range(3, NV)):
                    cross_terms(i, j, c)
                split_state(i, half)

            def split_y(i, half):
                act.wait_ge(y_masked, 2 * i + half + 1)
                c = slice(half * HALF, (half + 1) * HALF)
                act.activation(y_hi[:, c, :], ym[:, c, :], ACT.Copy).then_inc(y_hi_ready, 1)

            act.wait_ge(const_ready, 2)
            preload(ACT.Sin)
            for u in range(U_SIN):
                weight_high(u)
            act.wait_ge(half_angle, 1)
            act.activation(small[4][:, 0:N], small[2][:, 0:N], ACT.Sin, scale=0.5).then_inc(half_sin, 1)
            act.activation(small[5][:, 0:N], small[3][:, 0:N], ACT.Sin, scale=-0.5,
                           bias=half_pi[0:H, :]).then_inc(half_sin, 1)
            for u in range(U_SIN, U_X0 - 2):
                weight_high(u)
            group_sincos(0)
            group_decay(0)
            for u in range(U_X0 - 2, U_X0):
                weight_high(u)
            split_u(0, 0)
            act.wait_ge(comb_ready, 1)
            for half in range(2):
                act.activation(tab[half * N:(half + 1) * N, 0, 0:TROW - 1], comb[0:N, half, 0, 0:TROW - 1],
                               ACT.Copy).then_inc(tab_loaded[0], 8)
            act.wait_ge(tab_loaded[0], 16)
            split_gf(0, 0)
            for u in range(U_X0, U_S0):
                weight_high(u)
            act.wait_ge(pad_stored, 16)
            copy_v(0)
            weight_high(U_S0)
            for c in range(1, NV):
                cross_terms(0, 0, c)
                if c < NV - 1:
                    weight_high(U_S0 + c)
                if c == 2:
                    split_state(0, 0)
            split_state(0, 1)
            split_u(1, 1)
            act.wait_ge(tab_loaded[1], 16)
            split_gf(1, 1)
            split_y(0, 0)
            split_y(0, 1)
            copy_v(1)
            act.wait_ge(conv_done, 2)
            split_u(2, 2)
            act.wait_ge(tab_loaded[2], 16)
            split_gf(2, 2)

            def head(i, j, t=None):
                if i_left(i, 1):
                    states(i + 1, j + 1, 0)
                    states(i + 1, j + 1, 1)
                act.wait_ge(below_ready, i + 1)
                act.activation(weight[:], below[:], ACT.Exp).then_inc(weight_ready, 1)
                if j == 0 and t is not None:
                    group_decay(t + 1)
                if i_left(i, 2):
                    act.wait_ge(s_lo_ready, 2 * i + 4)
                    copy_v(i + 2)
                if j == 0 and t is not None:
                    preload(ACT.Sin)
                act.wait_ge(hw_turned, i + 1)
                act.activation(hwt_hi[:], ps_h[:, 0:P], ACT.Copy).then_inc(hwt_hi_ready, 1)
                if i_left(i, 1):
                    split_y(i + 1, 0)
                if j == 0 and t is not None:
                    group_sincos(t + 1)
                    preload(ACT.Exp)
                if i_left(i, 1):
                    split_y(i + 1, 1)
                if i_left(i, 3):
                    act.wait_ge(conv_done, 2 * i + 4)
                    split_u(i + 3, j + 3)
                    loads = 16 * (H // UNROLL) if t is None else 16 * t + 16 + 16 * ((j + 3) // UNROLL)
                    act.wait_ge(tab_loaded[(j + 3) % UNROLL], loads)
                    split_gf(i + 3, j + 3)

            with act.Fori(0, H // UNROLL - 1) as t:
                for j in range(UNROLL):
                    head(UNROLL * t + j, j, t)
            for i in range(H - UNROLL, H):
                head(i, i % UNROLL)

        @block.vector
        def _(dve):
            count = [0]

            def settle(behind):
                if count[0] > behind:
                    dve.wait_ge(dve_chain, count[0] - behind)

            def link(ins):
                count[0] += 1
                ins.then_inc(dve_chain, 1)

            def ts(o, i, s1, s2, op0, op1, behind=0):
                settle(behind)
                link(dve.tensor_scalar(o, i, s1, s2, op0, op1))

            def tt(o, a, b, op, behind=0):
                settle(behind)
                link(dve.tensor_tensor(o, a, b, op))

            def stt(o, a, s, b, op0, op1, behind=0):
                settle(behind)
                link(dve.scalar_tensor_tensor(out=o, in0=a, scalar=s, in1=b, op0=op0, op1=op1))

            EXP_STEPS = 14

            def exp_step(n, v, width, k, r, p, behind):
                if n == 0:
                    ts(r, v, -87.0, 88.0, ALU.max, ALU.min, behind)
                elif n == 1:
                    ts(k, r, LOG2E, MAGIC, ALU.mult, ALU.add, behind)
                elif n == 2:
                    ts(k, k, -MAGIC, None, ALU.add, ALU.bypass, behind)
                elif n == 3:
                    stt(r, k, -LN2_HI, r, ALU.mult, ALU.add, behind)
                elif n == 4:
                    stt(r, k, -LN2_LO, r, ALU.mult, ALU.add, behind)
                elif n == 5:
                    ts(p, r, 1.0 / 5040, None, ALU.mult, ALU.bypass, behind)
                elif n < 12:
                    stt(p, p, 1.0 / math.factorial(12 - n), r, ALU.add, ALU.mult, behind)
                elif n == 12:
                    ts(ki[:, 0:width], k, 127.0, 2.0 ** 23, ALU.add, ALU.mult, behind)
                else:
                    tt(p, p, ki[:, 0:width].bitcast(F32), ALU.mult, behind)

            def magnitude(dst, src):
                return dve.scalar_tensor_tensor(out=dst, in0=src, scalar=-1.0, in1=src, op0=ALU.mult, op1=ALU.max)

            def angle_step(g, n, first=False):
                wide = [P, GP, NPOS]
                if 1 < n < 8:
                    dve.wait_ge(gen_chain, GEN_STEPS * g + n - 1)
                if n == 0:
                    if not first:
                        dve.wait_ge(comb_ready, g)
                    dve.tensor_copy(cur[:], coef[:, :, bass.ds(GP * g, GP)]).then_inc(cur_ready, 1)
                elif n == 1:
                    dve.wait_ge(cur_ready, g + 1)
                    dve.tensor_tensor(theta[:], cur[:, 1, :].unsqueeze(2).broadcast_to(wide),
                                      pos[:].unsqueeze(1).broadcast_to(wide), ALU.mult).then_inc(gen_chain, 1)
                elif n == 2:
                    dve.tensor_scalar(turns[:], theta[:], 1 / (2 * math.pi), MAGIC, ALU.mult,
                                      ALU.add).then_inc(gen_chain, 1)
                elif n == 3:
                    dve.tensor_scalar(turns[:], turns[:], -MAGIC, None, ALU.add, ALU.bypass).then_inc(gen_chain, 1)
                elif n < 7:
                    part = (TWO_PI_1, TWO_PI_2, TWO_PI_3)[n - 4]
                    dve.scalar_tensor_tensor(out=theta[:], in0=turns[:], scalar=-part, in1=theta[:], op0=ALU.mult,
                                             op1=ALU.add).then_inc(gen_chain, 1)
                elif n == 7:
                    dve.tensor_scalar(theta[:], theta[:], -PI_BELOW, PI_BELOW, ALU.max,
                                      ALU.min).then_inc(angle_ready, 1)
                else:
                    dve.wait_ge(angle_ready, 2 * g + 1)
                    magnitude(turns[:], theta[:]).then_inc(angle_ready, 1)

            def k_step(g, n, sums=k_bank):
                if n == 0:
                    dve.wait_ge(k_summed, g + 1)
                    dve.tensor_copy(k_full[:], sums.rearrange(chunked, c=GP)).then_inc(ksum_chain, 1)
                elif n == 1:
                    dve.wait_ge(ksum_chain, KSUM_STEPS * g + 1)
                    dve.tensor_tensor(k_full[:, :, 0], k_full[:, :, 0], d_rows[:, bass.ds(GP * g, GP)],
                                      ALU.add).then_inc(ksum_chain, 1)
                elif n == 2:
                    dve.wait_ge(ksum_chain, KSUM_STEPS * g + 2)
                    dve.tensor_copy(k_split[:, 0, :, :], k_full[:]).then_inc(k_ready, 1)
                else:
                    dve.wait_ge(k_ready, 2 * g + 1)
                    dve.tensor_tensor(k_split[:, 1, :, :], k_full[:], k_split[:, 0, :, :].bitcast(F32),
                                      ALU.subtract).then_inc(k_ready, 1)

            def weight_low(u):
                dve.wait_ge(wt_hi_ready, u + 1)
                src, hi, lo, factor = unit_views(u)
                dve.scalar_tensor_tensor(out=lo, in0=src, scalar=factor, in1=hi.bitcast(F32),
                                         op0=ALU.mult, op1=ALU.subtract).then_inc(dve_low, 1)

            def split_u(i, j):
                for half in range(2):
                    dve.wait_ge(u_hi_ready, 2 * i + half + 1)
                    c = slice(half * HALF, (half + 1) * HALF)
                    dve.tensor_tensor(u_lo[:, j % 2, c, :], ps_u[half][:].rearrange(chunked, c=HALF),
                                      u_hi[:, j % 2, c, :].bitcast(F32), ALU.subtract).then_inc(u_lo_ready, 1)

            def split_g(i):
                dve.wait_ge(gf_hi_ready, 2 * i + 1)
                dve.tensor_tensor(g_lo[:], ps_h[:, 0:P], g_hi[:].bitcast(F32), ALU.subtract).then_inc(g_lo_ready, 1)

            def states(i, j, half, g=None, unit=None):
                for c in ((1, 2) if half == 0 else range(3, NV)):
                    at = STATE_STEPS * i + 2 * (c - 1)
                    if c == 1:
                        dve.wait_ge(v_copied, i + 1)
                    else:
                        dve.wait_ge(state_chain, at)
                    dve.scalar_tensor_tensor(out=state[:, c, :], in0=state[:, c - 1, :],
                                             scalar=tab[:, j % UNROLL, LAM_RE:LAM_RE + 1], in1=state[:, c, :],
                                             op0=ALU.mult, op1=ALU.add).then_inc(state_chain, 1)
                    if unit is not None:
                        weight_low(unit + c - 1)
                    if g is not None and j == 1:
                        for n in ANGLES_AT[c]:
                            angle_step(g, n)
                    if g is not None and j == 3:
                        for n in K_AT[c]:
                            k_step(g, n)
                    dve.wait_ge(state_chain, at + 1)
                    dve.wait_ge(cross_ready, (NV - 1) * i + c)
                    dve.tensor_tensor(state[:, c, :], state[:, c, :], cross[:], ALU.add).then_inc(state_chain, 1)

            def mask_y(i, half):
                dve.wait_ge(conv_done, 2 * i + half + 1)
                c = slice(half * HALF, (half + 1) * HALF)
                dve.tensor_tensor(ym[:, c, :], ps_y[half][:].rearrange(chunked, c=HALF),
                                  mask_cols[:, c, :], ALU.mult).then_inc(y_masked, 1)

            def route(i):
                done = [0]

                def then(ins):
                    done[0] += 1
                    ins.then_inc(route_chain, 1)
                    dve.wait_ge(route_chain, ROUTE_STEPS * i + done[0])

                dve.wait_ge(h_done, i + 1)
                dve.tensor_copy(logit[:], ps_base[2][:, R0:R0 + E])
                then(dve.tensor_reduce(top[:], ps_base[2][:, R0:R0 + E], AX_X, ALU.max))
                dve.tensor_scalar(below[:], logit[:], top[:, 0:1], None, ALU.subtract).then_inc(below_ready, 1)
                then(dve.tensor_tensor(before[:], logit[:].unsqueeze(1).broadcast_to([P, E, E]),
                                       logit[:].unsqueeze(2).broadcast_to([P, E, E]), ALU.is_ge))
                then(dve.tensor_tensor(before[:], before[:], lower[:], ALU.mult))
                then(dve.tensor_tensor(balance[:], before[:], before[:].rearrange("p e f -> p f e"), ALU.subtract))
                then(dve.tensor_reduce(rank[:], balance[:], AX_X, ALU.add))
                then(dve.tensor_tensor(gate[:], rank[:], rank_limit[:], ALU.is_lt))
                dve.wait_ge(weight_ready, i + 1)
                then(dve.tensor_tensor(gate[:], gate[:], weight[:], ALU.mult))
                then(dve.tensor_reduce(total[:], gate[:], AX_X, ALU.add))
                then(dve.reciprocal(total[:], total[:]))
                assert done[0] == ROUTE_STEPS
                dve.scalar_tensor_tensor(out=hw[:], in0=ps_base[2][:, A0:A0 + ER].rearrange("p (e r) -> p e r", e=E),
                                         scalar=total[:, 0:1], in1=gate[:].unsqueeze(2).broadcast_to([P, E, R]),
                                         op0=ALU.mult, op1=ALU.mult).then_inc(hw_ready, 1)

            def split_hw(i):
                dve.wait_ge(hwt_hi_ready, i + 1)
                dve.tensor_tensor(hwt_lo[:], ps_h[:, 0:P], hwt_hi[:].bitcast(F32),
                                  ALU.subtract).then_inc(hwt_lo_ready, 1)

            def sum_out(i, j, s_):
                if s_ == 0:
                    dve.wait_ge(x_biased, i + 1)
                dve.wait_ge(lora_done, 3 * i + s_ + 1)
                a, b = LSEG[s_], LSEG[s_ + 1]
                dve.tensor_tensor(x_slot[:, j, a:b], ps_base[s_][:, 0:b - a], x_slot[:, j, a:b],
                                  ALU.add).then_inc(out_ready[s_], 1)

            dve.wait_ge(lin_in, 32)
            s = [v[:, 0:N] for v in small]
            ex = small[6]
            for n in range(EXP_STEPS):
                exp_step(n, lin[:], N + 1, small[0][:], small[1][:], small[7][:], 0)
            tt(ex[:], small[7][:], ki[:].bitcast(F32), ALU.add)
            mag, dt = ex[:, 0:N], ex[:, N:N + 1]
            a_nat, w_nat = nat[:, 0, 0, :], nat[:, 1, 0, :]
            angle, quot, inv, em1 = s[2], s[3], s[9], s[8]
            settle(0)
            dve.wait_ge(aim_c_in, 32)
            ts(angle, aim[:], dt, None, ALU.mult, ALU.bypass, 1)
            ts(a_nat, mag, dt, -1.0, ALU.mult, ALU.mult, 1)
            ts(w_nat, aim[:], dt, None, ALU.mult, ALU.bypass, 1)
            for n in range(EXP_STEPS):
                exp_step(n, a_nat, N, s[0], s[1], s[7], 1 if n < 13 else 0)
                if n == 0:
                    ts(quot, angle, 1 / (2 * math.pi), MAGIC, ALU.mult, ALU.add, 1)
                elif n == 1:
                    ts(quot, quot, -MAGIC, None, ALU.add, ALU.bypass, 1)
                elif n < 5:
                    stt(angle, quot, -(TWO_PI_1, TWO_PI_2, TWO_PI_3)[n - 2], angle, ALU.mult, ALU.add, 1)
                elif n == 5:
                    ts(angle, angle, -PI_BELOW, PI_BELOW, ALU.max, ALU.min, 1)
                elif n == 6:
                    settle(1)
                    magnitude(quot, angle).then_inc(half_angle, 1)
                    dve.wait_ge(half_angle, 1)
                elif n == 7:
                    tt(inv, mag, mag, ALU.mult, 1)
                elif n == 8:
                    tt(em1, aim[:], aim[:], ALU.mult, 1)
                elif n == 9:
                    tt(inv, inv, em1, ALU.add, 0)
                elif n == 10:
                    settle(1)
                    link(dve.reciprocal(inv, inv))
            stt(em1, ki[:, 0:N].bitcast(F32), -1.0, s[7], ALU.add, ALU.add, 0)
            dve.wait_ge(half_sin, 2)
            sn, cs = s[4], s[5]
            c_re, c_im = cc[:, :, 0], cc[:, :, 1]
            tt(s[0], sn, sn, ALU.mult, 1)
            tt(s[2], sn, cs, ALU.mult, 1)
            ts(s[0], s[0], -2.0, None, ALU.mult, ALU.bypass, 1)
            stt(s[2], em1, 1.0, s[2], ALU.add, ALU.mult, 1)
            stt(s[1], s[0], 1.0, em1, ALU.add, ALU.mult, 1)
            ts(s[2], s[2], 2.0, None, ALU.mult, ALU.bypass, 1)
            tt(s[1], s[1], s[0], ALU.add, 1)
            tt(s[4], c_im, s[2], ALU.mult, 1)
            tt(s[3], c_re, s[1], ALU.mult, 1)
            tt(s[7], c_re, s[2], ALU.mult, 1)
            tt(s[5], c_im, s[1], ALU.mult, 1)
            tt(s[3], s[3], s[4], ALU.subtract, 1)
            tt(s[7], s[7], s[5], ALU.add, 1)
            tt(s[2], s[3], mag, ALU.mult, 1)
            tt(s[1], s[7], aim[:], ALU.mult, 1)
            tt(s[4], s[3], aim[:], ALU.mult, 1)
            tt(s[5], s[7], mag, ALU.mult, 1)
            tt(s[1], s[1], s[2], ALU.subtract, 1)
            stt(s[4], s[4], -1.0, s[5], ALU.mult, ALU.subtract, 1)
            stt(nat[:, 2, 0, :], s[1], 2.0, inv, ALU.mult, ALU.mult, 1)
            stt(nat[:, 3, 0, :], s[4], 2.0, inv, ALU.mult, ALU.mult, 1)
            stt(nat[:, 4, 0, :], s[1], -2.0, inv, ALU.mult, ALU.mult, 1)
            settle(0)
            dve.tensor_copy(nat[:, :, 1, :], nat[:, :, 0, :]).then_inc(nat_ready, 1)
            dve.wait_ge(nat_turned, 1)
            turned = ps_h[:, 0:5 * H].rearrange("p (k h two) -> p k h two", k=5, two=2)
            dve.tensor_copy(coef[0:N, :, :], turned[0:N, :, :, 0]).then_inc(coef_ready, 1)
            dve.tensor_copy(coef[N:P, :, :], turned[N:P, :, :, 1]).then_inc(coef_ready, 1)
            dve.wait_ge(coef_ready, 2)
            dve.wait_ge(const_ready, 6)
            for n in range(ANGLE_STEPS):
                angle_step(0, n, first=True)
            for u in range(POOL_UNITS, POOL_UNITS + 3):
                weight_low(u)
            tables(dve, 0, first=True)
            split_u(0, 0)
            split_g(0)
            dve.wait_ge(d_in, 16)
            for n in range(K_STEPS):
                k_step(0, n, ps_y[0][0:2, 0:GP * P])
            for u in range(POOL_UNITS + 3, U_S0):
                weight_low(u)
            states(0, 0, 0, unit=U_S0)
            low_states(dve, 0, 0)
            states(0, 0, 1, unit=U_S0)
            dve.wait_ge(masks_ready, NC)
            mask_y(0, 0)
            split_u(1, 1)
            split_g(1)
            low_y(dve, 0, 0)
            mask_y(0, 1)
            split_u(2, 2)
            split_g(2)

            def head(i, j, t=None):
                g = None if t is None else t + 1
                if i_left(i, 1):
                    states(i + 1, j + 1, 0, g)
                    states(i + 1, j + 1, 1, g)
                if j == 0 and t is not None:
                    angle_step(g, 8)
                route(i)
                if i_left(i, 1):
                    mask_y(i + 1, 0)
                split_hw(i)
                if i_left(i, 1):
                    low_y(dve, i + 1, 0)
                sum_out(i, j, 0)
                if i_left(i, 1):
                    mask_y(i + 1, 1)
                sum_out(i, j, 1)
                sum_out(i, j, 2)
                if i_left(i, 3):
                    split_u(i + 3, j + 3)
                    split_g(i + 3)

            with dve.Fori(0, H // UNROLL - 1) as t:
                for j in range(UNROLL):
                    head(UNROLL * t + j, j, t)
            for i in range(H - UNROLL, H):
                head(i, i % UNROLL)

        @block.tensor
        def _(pe):
            def turn_x(i):
                pe.wait_ge(x_masked, i + 1)
                for half in range(2):
                    for k in range(HALF):
                        c = half * HALF + k
                        mm = pe.transpose(ps_u[half][:, k * P:(k + 1) * P], xm[:, c * P:(c + 1) * P], ident[:])
                    mm.then_inc(u_turned, 1)

            def turn_g(i, j, loads):
                pe.wait_ge(tab_loaded[j % UNROLL], loads)
                pe.transpose(ps_h[:, 0:P], tab[:, j % UNROLL, 0:P], ident[:]).then_inc(g_turned, 1)

            def input_product(i, j):
                pe.wait_ge(u_lo_ready, 2 * i + 2)
                pe.wait_ge(g_lo_ready, i + 1)
                for half in range(2):
                    a, b = half * HALF, min((half + 1) * HALF, NV)
                    for n, (g, u) in enumerate(((g_hi, u_hi), (g_hi, u_lo), (g_lo, u_hi))):
                        mm = pe.matmul(ps_u[half][:, 0:(b - a) * P], g[:], u[:, j % 2, a:b, :],
                                       start=(n == 0), stop=(n == 2))
                mm.then_inc(v_done, 1)

            def conv(i, j, half):
                c = slice(half * HALF, (half + 1) * HALF)
                for n, (part, u) in enumerate(((0, u_hi), (0, u_lo), (1, u_hi))):
                    pe.matmul(ps_y[half][:], toep[:, j % UNROLL, part, :], u[:, j % 2, c, :],
                              start=(n == 0), stop=False)
                a, b = (0, HALF - 1) if half == 0 else (HALF - 1, NV)
                if half == 0:
                    pe.wait_ge(f_lo_ready, i + 1)
                pe.wait_ge(s_lo_ready, 2 * i + half + 1)
                for n, (f, s) in enumerate(((f_hi, s_hi), (f_hi, s_lo), (f_lo, s_hi))):
                    mm = pe.matmul(ps_y[half][:, BANK - (b - a) * P:BANK], f[:, j % 2, :], s[:, a:b, :],
                                   start=False, stop=(n == 2))
                mm.then_inc(conv_done, 1)

            def linear(chunks, pieces):
                for s in pieces:
                    for c in chunks:
                        for n, (y, w) in enumerate(((y_hi, w_hi), (y_hi, w_lo), (y_lo, w_hi))):
                            mm = pe.matmul(ps_base[s][:, 0:SEG[s + 1] - SEG[s]], y[:, c, :],
                                           w[:, c, SEG[s]:SEG[s + 1]], start=(c == 0 and n == 0),
                                           stop=(c == NC - 1 and n == 2))
                return mm

            def linear_start(i):
                pe.wait_ge(y_lo_ready[0], i + 1)
                for s in range(3):
                    pe.wait_ge(out_ready[s], i)
                    linear(range(2), [s])

            def turn_hw(i):
                pe.wait_ge(hw_ready, i + 1)
                pe.transpose(ps_h[:, 0:P], hw[:].rearrange("p e r -> p (e r)"), ident[:]).then_inc(hw_turned, 1)

            def lora(i):
                pe.wait_ge(hwt_lo_ready, i + 1)
                for s in range(3):
                    a, b = LSEG[s], LSEG[s + 1]
                    for n, (h, w) in enumerate(((hwt_hi, b2_hi), (hwt_hi, b2_lo), (hwt_lo, b2_hi))):
                        mm = pe.matmul(ps_base[s][:, 0:b - a], h[:], w[:, a:b], start=False, stop=(n == 2),
                                       skip_group_check=True)
                    mm.then_inc(lora_done, 1)

            def sum_k(g, sums=k_bank):
                pe.wait_ge(comb_ready, g + 1)
                pe.matmul(sums, parity[:], comb[:, 0, :, FCOL:FCOL + P], start=True,
                          stop=True).then_inc(k_summed, 1)

            pe.wait_ge(const_ready, 1)
            for u in range(U_NAT):
                weight_unit(pe, u)
            pe.wait_ge(nat_ready, 1)
            for k in range(5):
                mm = pe.transpose(ps_h[:, k * H:(k + 1) * H], nat[:, k, :, :].rearrange("h two n -> h (two n)"),
                                  ident[0:H, 0:H])
            mm.then_inc(nat_turned, 1)
            for u in range(U_NAT, U_X0):
                weight_unit(pe, u)
            turn_x(0)
            pe.wait_ge(const_ready, 6)
            sum_k(0, ps_y[0][0:2, 0:GP * P])
            turn_g(0, 0, 16)
            for u in range(U_X0, U_S0):
                weight_unit(pe, u)
            input_product(0, 0)
            for u in range(U_S0, NUNITS - 2):
                weight_unit(pe, u)
            pe.wait_ge(v_copied, 1)
            turn_x(1)
            turn_g(1, 1, 16)
            for u in range(NUNITS - 2, NUNITS):
                weight_unit(pe, u)
            pe.wait_ge(k_ready, 2)
            pe.wait_ge(toep_loaded[0], 16)
            conv(0, 0, 0)
            pe.wait_ge(pool_low, POOL_UNITS)
            pe.wait_ge(dve_low, NUNITS - POOL_UNITS)
            conv(0, 0, 1)
            input_product(1, 1)
            pe.wait_ge(y_lo_ready[0], 1)
            linear(range(2), [0])
            pe.wait_ge(v_copied, 2)
            turn_x(2)
            turn_g(2, 2, 16)
            linear(range(2), [1, 2])

            def head(i, j, t=None):
                def loads(ahead):
                    return 16 * (H // UNROLL) if t is None else 16 * t + 16 + 16 * ((j + ahead) // UNROLL)

                linear(range(2, HALF), [0])
                if j == 2 and t is not None:
                    pe.wait_ge(g_lo_ready, i + 3)
                    sum_k(t + 1)
                linear(range(2, HALF), [1, 2])
                pe.wait_ge(y_lo_ready[1], i + 1)
                linear(range(HALF, NC), [2]).then_inc(h_done, 1)
                if i_left(i, 2):
                    input_product(i + 2, j + 2)
                linear(range(HALF, NC), [0])
                linear(range(HALF, NC - 2), [1])
                if not i_left(i, 1):
                    turn_hw(i)
                linear(range(NC - 2, NC), [1])
                if j == 2 and t is not None:
                    pe.wait_ge(k_ready, 2 * t + 3)
                if i_left(i, 1):
                    pe.wait_ge(toep_loaded[(j + 1) % UNROLL], loads(1))
                    conv(i + 1, j + 1, 0)
                    turn_hw(i)
                    conv(i + 1, j + 1, 1)
                lora(i)
                if i_left(i, 3):
                    pe.wait_ge(v_copied, i + 3)
                    turn_x(i + 3)
                    turn_g(i + 3, j + 3, loads(3))
                if i_left(i, 1):
                    linear_start(i + 1)

            with pe.Fori(0, H // UNROLL - 1) as t:
                for j in range(UNROLL):
                    head(UNROLL * t + j, j, t)
            for i in range(H - UNROLL, H):
                head(i, i % UNROLL)


_INS = ['x', 'itok_B_8_3872', 'L0_cond_log_dt', 'L0_cond_C', 'L0_cond_log_A_real', 'L0_cond_A_imag', 'L0_cond_D',
        'L0_ffn_W_base', 'L0_ffn_b_base', 'L0_ffn_W_router', 'L0_ffn_A', 'L0_ffn_B']


def kernel(**inputs):
    import concourse.bacc as _bacc
    from concourse.bass_utils import run_bass_kernel_spmd as _run

    nc = _bacc.Bacc("TRN2", target_bir_lowering=False, num_devices=1)
    arrays, args = {}, []
    for name in _INS:
        a = np.ascontiguousarray(inputs[name])
        arrays[f"in_{name}_dram"] = a
        args.append(nc.dram_tensor(f"in_{name}_dram", a.shape, mybir.dt.from_np(a.dtype), kind="ExternalInput").ap())
    args.append(nc.dram_tensor("out_0_dram", inputs['x'].shape, F32, kind="ExternalOutput").ap())
    s4d_lora_ffn(nc, *args)
    r = _run(nc, [arrays], core_ids=[0])
    return r.results[0]["out_0_dram"]
```
